# Optimizing a Trainium2 kernel written in Bass

```python
import numpy as np
import jax
import jax.numpy as jnp

def _softmax(x, axis=-1):
    return jax.nn.softmax(x, axis=axis)

def _gelu(x):
    return jax.nn.gelu(x, approximate=True)

def _silu(x):
    return jax.nn.silu(x)

def _sigmoid(x):
    return jax.nn.sigmoid(x)

def _layernorm(x, axis=-1, eps=1e-05):
    m = jnp.mean(x, axis=axis, keepdims=True)
    v = jnp.var(x, axis=axis, keepdims=True)
    return (x - m) / jnp.sqrt(v + eps)

def _scatter_add(tgt, idx, src, axis=0):
    return tgt.at[idx].add(src)

def _segment_sum(src, seg, n):
    return jax.ops.segment_sum(src, seg, n)
kernel_name = 'mk_seq_postln_d2_jaxref_r8_ca095e'

def setup_inputs(seed: int=0):
    np.random.seed(seed)
    _w = jnp.asarray

    def _L0_attn_setup():
        import jax, jax.numpy as jnp
        import numpy as np
        import math
        EMBED_DIM = 128
        NUM_HEADS = 16
        HEAD_DIM = EMBED_DIM // NUM_HEADS
        MAX_LEN = 625
        LN_EPS = 1e-05

        def _positional_encoding(max_len, embed_dim):
            pos = np.arange(max_len, dtype=np.float32)[:, None]
            div = np.exp(np.arange(0, embed_dim, 2, dtype=np.float32) * (-math.log(10000.0) / embed_dim))
            pe = np.zeros((max_len, embed_dim), dtype=np.float32)
            pe[:, 0::2] = np.sin(pos * div)
            pe[:, 1::2] = np.cos(pos * div)
            return jnp.asarray(pe)[None]
        key = jax.random.key(seed)
        ks = jax.random.split(key, 12)
        s = 1.0 / math.sqrt(EMBED_DIM)
        D = EMBED_DIM
        return {'x': jax.random.normal(ks[0], (4, 256, D), dtype=jnp.float32), 'wq': jax.random.uniform(ks[1], (D, D), jnp.float32, -s, s), 'bq': jax.random.uniform(ks[2], (D,), jnp.float32, -s, s), 'wk': jax.random.uniform(ks[3], (D, D), jnp.float32, -s, s), 'bk': jax.random.uniform(ks[4], (D,), jnp.float32, -s, s), 'wv': jax.random.uniform(ks[5], (D, D), jnp.float32, -s, s), 'bv': jax.random.uniform(ks[6], (D,), jnp.float32, -s, s), 'wo': jax.random.uniform(ks[7], (D, D), jnp.float32, -s, s), 'bo': jax.random.uniform(ks[8], (D,), jnp.float32, -s, s), 'gamma': jnp.ones((D,), jnp.float32), 'beta': jnp.zeros((D,), jnp.float32), 'pe': _positional_encoding(MAX_LEN, D)}
    _L0_attn_in = _L0_attn_setup()

    def _L0_ffn_setup():
        import jax, jax.numpy as jnp
        import numpy as np
        EPS = 1e-09
        key = jax.random.key(seed)
        k0, k1, k2, k3 = jax.random.split(key, 4)
        B, S, H, F, E = (4, 256, 128, 256, 8)
        return {'hidden_states': jax.random.normal(k0, (B, S, H), dtype=jnp.float32), 'router_w': jax.random.normal(k1, (H, E), dtype=jnp.float32) * 0.02, 'w1': jax.random.normal(k2, (E, H, F), dtype=jnp.float32) * 0.02, 'w2': jax.random.normal(k3, (E, F, H), dtype=jnp.float32) * 0.02}
    _L0_ffn_in = _L0_ffn_setup()

    def _L1_attn_setup():
        import jax, jax.numpy as jnp
        import numpy as np
        N_HEADS = 16
        HEAD_DIM = 64
        ROPE_THETA = 10000.0

        def _rope_cos_sin(seq_len, dim, theta):
            inv_freq = 1.0 / theta ** (jnp.arange(0, dim, 2, dtype=jnp.float32) / dim)
            pos = jnp.arange(seq_len, dtype=jnp.float32)
            freqs = pos[:, None] * inv_freq[None, :]
            emb = jnp.concatenate([freqs, freqs], axis=-1)
            return (jnp.cos(emb), jnp.sin(emb))

        def _rotate_half(x):
            d = x.shape[-1] // 2
            return jnp.concatenate([-x[..., d:], x[..., :d]], axis=-1)
        key = jax.random.key(seed)
        ks = jax.random.split(key, 6)
        B, S, D_MODEL, LATENT = (1, 512, 128, 64)
        q_dim = N_HEADS * HEAD_DIM
        sd = lambda fan_in: 1.0 / np.sqrt(fan_in)
        return {'x': jax.random.normal(ks[0], (B, S, D_MODEL), jnp.float32), 'wq': jax.random.normal(ks[1], (q_dim, D_MODEL), jnp.float32) * sd(D_MODEL), 'w_kv_down': jax.random.normal(ks[2], (LATENT, D_MODEL), jnp.float32) * sd(D_MODEL), 'w_k_up': jax.random.normal(ks[3], (q_dim, LATENT), jnp.float32) * sd(LATENT), 'w_v_up': jax.random.normal(ks[4], (q_dim, LATENT), jnp.float32) * sd(LATENT), 'wo': jax.random.normal(ks[5], (D_MODEL, q_dim), jnp.float32) * sd(q_dim)}
    _L1_attn_in = _L1_attn_setup()

    def _L1_ffn_setup():
        import jax, jax.numpy as jnp
        import numpy as np
        NUM_GEMMS = 8
        HIDDEN = 128
        INTER = 512
        key = jax.random.key(seed)
        k_x, k_w1, k_b1, k_w2, k_b2 = jax.random.split(key, 5)
        x = jax.random.normal(k_x, (8, 256, HIDDEN), dtype=jnp.float32)
        s1 = 1.0 / np.sqrt(HIDDEN)
        s2 = 1.0 / np.sqrt(INTER)
        W1 = jax.random.uniform(k_w1, (NUM_GEMMS, INTER, HIDDEN), jnp.float32, -s1, s1)
        b1 = jax.random.uniform(k_b1, (NUM_GEMMS, INTER), jnp.float32, -s1, s1)
        W2 = jax.random.uniform(k_w2, (NUM_GEMMS, HIDDEN, INTER), jnp.float32, -s2, s2)
        b2 = jax.random.uniform(k_b2, (NUM_GEMMS, HIDDEN), jnp.float32, -s2, s2)
        return {'x': x, 'W1': W1, 'b1': b1, 'W2': W2, 'b2': b2}
    _L1_ffn_in = _L1_ffn_setup()
    _d = {'L0_attn_x': _L0_attn_in['x'], 'L0_attn_wq': _L0_attn_in['wq'], 'L0_attn_bq': _L0_attn_in['bq'], 'L0_attn_wk': _L0_attn_in['wk'], 'L0_attn_bk': _L0_attn_in['bk'], 'L0_attn_wv': _L0_attn_in['wv'], 'L0_attn_bv': _L0_attn_in['bv'], 'L0_attn_wo': _L0_attn_in['wo'], 'L0_attn_bo': _L0_attn_in['bo'], 'L0_attn_gamma': _L0_attn_in['gamma'], 'L0_attn_beta': _L0_attn_in['beta'], 'L0_attn_pe': _L0_attn_in['pe'], 'L0_ffn_router_w': _L0_ffn_in['router_w'], 'L0_ffn_w1': _L0_ffn_in['w1'], 'L0_ffn_w2': _L0_ffn_in['w2'], 'L1_attn_wq': _L1_attn_in['wq'], 'L1_attn_w_kv_down': _L1_attn_in['w_kv_down'], 'L1_attn_w_k_up': _L1_attn_in['w_k_up'], 'L1_attn_w_v_up': _L1_attn_in['w_v_up'], 'L1_attn_wo': _L1_attn_in['wo'], 'L1_ffn_W1': _L1_ffn_in['W1'], 'L1_ffn_b1': _L1_ffn_in['b1'], 'L1_ffn_W2': _L1_ffn_in['W2'], 'L1_ffn_b2': _L1_ffn_in['b2']}
    _x0 = _d['L0_attn_x']
    _d['L0_attn_x'] = jax.random.normal(jax.random.fold_in(jax.random.key(seed), 1), (8, 256, 128), dtype=_x0.dtype)
    del _x0
    return _d

def reference(L0_attn_x, L0_attn_wq, L0_attn_bq, L0_attn_wk, L0_attn_bk, L0_attn_wv, L0_attn_bv, L0_attn_wo, L0_attn_bo, L0_attn_gamma, L0_attn_beta, L0_attn_pe, L0_ffn_router_w, L0_ffn_w1, L0_ffn_w2, L1_attn_wq, L1_attn_w_kv_down, L1_attn_w_k_up, L1_attn_w_v_up, L1_attn_wo, L1_ffn_W1, L1_ffn_b1, L1_ffn_W2, L1_ffn_b2):

    def _L0_attn_ref(x, wq, bq, wk, bk, wv, bv, wo, bo, gamma, beta, pe):
        import jax, jax.numpy as jnp
        import numpy as np
        import math
        EMBED_DIM = 128
        NUM_HEADS = 16
        HEAD_DIM = EMBED_DIM // NUM_HEADS
        MAX_LEN = 625
        LN_EPS = 1e-05

        def _positional_encoding(max_len, embed_dim):
            pos = np.arange(max_len, dtype=np.float32)[:, None]
            div = np.exp(np.arange(0, embed_dim, 2, dtype=np.float32) * (-math.log(10000.0) / embed_dim))
            pe = np.zeros((max_len, embed_dim), dtype=np.float32)
            pe[:, 0::2] = np.sin(pos * div)
            pe[:, 1::2] = np.cos(pos * div)
            return jnp.asarray(pe)[None]
        B, S, D = x.shape
        H, Hd = (NUM_HEADS, HEAD_DIM)
        x = x + pe[:, :S, :]
        q = (x @ wq + bq).reshape(B, S, H, Hd).transpose(0, 2, 1, 3)
        k = (x @ wk + bk).reshape(B, S, H, Hd).transpose(0, 2, 1, 3)
        v = (x @ wv + bv).reshape(B, S, H, Hd).transpose(0, 2, 1, 3)
        scores = jnp.einsum('bhqd,bhkd->bhqk', q, k) / math.sqrt(Hd)
        attn = jax.nn.softmax(scores, axis=-1)
        out = jnp.einsum('bhqk,bhkd->bhqd', attn, v)
        out = out.transpose(0, 2, 1, 3).reshape(B, S, D)
        out = out @ wo + bo
        h = out + x
        mu = jnp.mean(h, axis=-1, keepdims=True)
        var = jnp.var(h, axis=-1, keepdims=True)
        return (h - mu) * jax.lax.rsqrt(var + LN_EPS) * gamma + beta

    def _L0_ffn_ref(hidden_states, router_w, w1, w2):
        import jax, jax.numpy as jnp
        import numpy as np
        EPS = 1e-09
        TOP_K = 2
        orig_shape = hidden_states.shape
        H = orig_shape[-1]
        E = router_w.shape[-1]
        flat = hidden_states.reshape(-1, H)
        T = flat.shape[0]
        gate_logits = flat @ router_w
        gate_probs = jax.nn.softmax(gate_logits, axis=-1)
        topk_w, topk_idx = jax.lax.top_k(gate_probs, TOP_K)
        topk_w = topk_w / jnp.clip(topk_w.sum(-1, keepdims=True), EPS)
        cw = jnp.zeros((T, E), dtype=flat.dtype).at[jnp.arange(T)[:, None], topk_idx].add(topk_w)
        h = jax.nn.silu(jnp.einsum('td,edf->etf', flat, w1))
        y = jnp.einsum('etf,efd->etd', h, w2)
        out = jnp.einsum('etd,te->td', y, cw)
        return out.reshape(orig_shape)

    def _L1_attn_ref(x, wq, w_kv_down, w_k_up, w_v_up, wo):
        import jax, jax.numpy as jnp
        import numpy as np
        N_HEADS = 16
        HEAD_DIM = 64
        ROPE_THETA = 10000.0

        def _rope_cos_sin(seq_len, dim, theta):
            inv_freq = 1.0 / theta ** (jnp.arange(0, dim, 2, dtype=jnp.float32) / dim)
            pos = jnp.arange(seq_len, dtype=jnp.float32)
            freqs = pos[:, None] * inv_freq[None, :]
            emb = jnp.concatenate([freqs, freqs], axis=-1)
            return (jnp.cos(emb), jnp.sin(emb))

        def _rotate_half(x):
            d = x.shape[-1] // 2
            return jnp.concatenate([-x[..., d:], x[..., :d]], axis=-1)
        B, S, _ = x.shape
        H, D = (N_HEADS, HEAD_DIM)
        q = jnp.einsum('bsd,qd->bsq', x, wq).reshape(B, S, H, D).transpose(0, 2, 1, 3)
        kv_latent = jnp.einsum('bsd,ld->bsl', x, w_kv_down)
        k = jnp.einsum('bsl,ql->bsq', kv_latent, w_k_up).reshape(B, S, H, D).transpose(0, 2, 1, 3)
        v = jnp.einsum('bsl,ql->bsq', kv_latent, w_v_up).reshape(B, S, H, D).transpose(0, 2, 1, 3)
        cos, sin = _rope_cos_sin(S, D, ROPE_THETA)
        cos = cos[None, None]
        sin = sin[None, None]
        q = q * cos + _rotate_half(q) * sin
        k = k * cos + _rotate_half(k) * sin
        scores = jnp.einsum('bhsd,bhtd->bhst', q, k) / jnp.sqrt(jnp.float32(D))
        causal = jnp.triu(jnp.full((S, S), -jnp.inf, dtype=jnp.float32), k=1)
        scores = scores + causal[None, None]
        probs = jax.nn.softmax(scores.astype(jnp.float32), axis=-1).astype(q.dtype)
        out = jnp.einsum('bhst,bhtd->bhsd', probs, v)
        out = out.transpose(0, 2, 1, 3).reshape(B, S, H * D)
        return jnp.einsum('bsq,dq->bsd', out, wo)

    def _L1_ffn_ref(x, W1, b1, W2, b2):
        import jax, jax.numpy as jnp
        import numpy as np
        NUM_GEMMS = 8
        HIDDEN = 128
        INTER = 512
        orig_shape = x.shape
        token_num = int(np.prod(orig_shape[:-1]))
        m = token_num // NUM_GEMMS
        xg = x.reshape(NUM_GEMMS, m, HIDDEN)
        h1 = jnp.einsum('gmh,goh->gmo', xg, W1) + b1[:, None, :]
        h2 = jnp.einsum('gmo,gho->gmh', h1, W2) + b2[:, None, :]
        return h2.reshape(orig_shape)
    x = L0_attn_x
    x = _layernorm(x + _L0_attn_ref(x, L0_attn_wq, L0_attn_bq, L0_attn_wk, L0_attn_bk, L0_attn_wv, L0_attn_bv, L0_attn_wo, L0_attn_bo, L0_attn_gamma, L0_attn_beta, L0_attn_pe), axis=-1)
    x = _layernorm(x + _L0_ffn_ref(x, L0_ffn_router_w, L0_ffn_w1, L0_ffn_w2), axis=-1)
    x = _layernorm(x + _L1_attn_ref(x, L1_attn_wq, L1_attn_w_kv_down, L1_attn_w_k_up, L1_attn_w_v_up, L1_attn_wo), axis=-1)
    x = _layernorm(x + _L1_ffn_ref(x, L1_ffn_W1, L1_ffn_b1, L1_ffn_W2, L1_ffn_b2), axis=-1)
    return x

_drawn_inputs = setup_inputs


def setup_inputs(seed=0):
    import zlib

    import numpy as np

    out = dict(_drawn_inputs(seed))
    spreads = {'L0_attn_gamma': (1.0, 0.2), 'L0_attn_beta': (0.0, 0.1)}
    factors = {'L0_attn_wq': 5.119, 'L0_attn_bq': 8.0, 'L0_attn_wk': 5.304, 'L0_attn_bk': 8.0}
    for name, (base, spread) in spreads.items():
        noise = np.random.default_rng([zlib.crc32(name.encode()), seed]).standard_normal(out[name].shape)
        drawn = base * np.exp(spread * noise) if base else spread * noise
        out[name] = jnp.asarray(drawn.astype(out[name].dtype))
    for name, factor in factors.items():
        out[name] = (out[name] * factor).astype(out[name].dtype)
    return out
```

```python
from contextlib import ExitStack

import numpy as np

import concourse.bass as bass
from concourse import mybir

F32 = mybir.dt.float32
F16 = mybir.dt.float16
I32 = mybir.dt.int32
ALU = mybir.AluOpType
ACT = mybir.ActivationFunctionType
AX = mybir.AxisListType

B, S, D = 8, 256, 128
P = 128
T = S // P
H = 16
HD0, HD1 = 8, 64
G = H // 4
E, FI = 8, 256
LAT = 64
OCH = 4
LN_EPS, GATE_EPS = 1e-5, 1e-9
SCALE0, SCALE1 = HD0 ** -0.5, HD1 ** -0.5
RSQRT_BITS = float(0x5F3759DF)
MASKED = -60000.0


def build(nc, a, out, VCH=120):
    ctx = ExitStack()
    with ctx:
        def sb(name, shape, dt=F32):
            return ctx.enter_context(nc.sbuf_tensor(name, shape, dt))

        def sem(name):
            return ctx.enter_context(nc.semaphore(name))

        x_sb = sb("x_sb", [P, B * T, D])
        xT_sb = sb("xT_sb", [P, B * S])
        pe_sb = sb("pe_sb", [P, T, D])
        peT_sb = sb("peT_sb", [P, S])
        names = {}
        for n, v in a.items():
            if n not in ("x", "xT", "pe", "peT", "w_kup", "w_vup", "w_o1", "w_kvd", "W1", "W2T", "b1", "b2", "wo0T_bias"):
                names[n] = sb("c_" + n, list(v.shape), v.dtype)
        c = names
        rot = sb("rot", [P, 4, 2, G * S])
        OL = sb("OL", [P, H // 2, S])
        W1 = rot[:, 0:2].rearrange("p a b (o n) -> p (a b o) n", n=D)
        W2T = rot[:, 2:4].rearrange("p a b (o n) -> p (a b o) n", n=D)
        kup = OL[0:LAT, 0:4].rearrange("p h n -> p (h n)")
        wo1 = OL[:, 4:8].rearrange("p h (a n) -> p (h a) n", n=D)
        kvd = sb("kvd", [LAT, D])
        vup = sb("vup", [P, H // 2, LAT])
        b1 = sb("b1", [P, B * OCH])
        b2 = sb("b2", [1, B * D])
        ones_row = sb("ones_row", [1, P])
        wk_eff = sb("wk_eff", [P, 2, G, P])
        vo = sb("vo", [P, H // 2, D])
        Wc = sb("Wc", [P, B, D])
        bc = sb("bc", [P, B, D])

        xeT = sb("xeT", [P, S])
        xe = sb("xe", [P, T, D])
        xb = sb("xb", [P, T, D])
        K4 = sb("K4", [96, G, S], F16)
        Q4 = sb("Q4", [P, G, S], F16)
        Km = sb("Km", [P, G, 4, S], F16)
        V0 = sb("V0", [P, T, H, 32])
        mx = sb("mx", [P, T, H])
        nm = sb("nm", [P, T, 32], F16)
        Pr = sb("Pr", [P, 4, 1024])
        U = Pr[:, 0]
        att = sb("att", [P, G * S])
        ln_s = sb("ln_s", [P, T, D])
        ln_t = sb("ln_t", [P, T, D])
        spare = sb("spare", [P, 1])
        st = sb("st", [P, T, 6])
        mv = sb("mv", [P, T, 2])
        rs = sb("rs", [P, T])
        rw = sb("rw", [P, T])
        wv = sb("wv", [P, T])
        x1 = sb("x1", [P, T, D])
        xnT = sb("xnT", [P, S])
        lg = sb("lg", [P, T, 8])
        lmx = sb("lmx", [P, T])
        ge = sb("ge", [P, T, 8])
        gp = sb("gp", [P, T, 16])
        top = sb("top", [P, T, 8])
        gr = sb("gr", [P, T, 16])
        gs = sb("gs", [P, T])
        cw = sb("cw", [P, T, 8])
        hT = sb("hT", [P, 2, 2, S])
        th = hT[:].rearrange("p e c s -> p e (c s)")
        y = sb("y", [P, 2, T, D])
        lat = sb("lat", [P, T, LAT])
        ones64 = sb("ones64", [P, LAT])
        rot8 = rot[:].rearrange("p a b n -> p (a b) n")
        kraw, kr, kt = rot8[:, 0:2], rot8[:, 2:4], rot8[:, 4]
        qr, qt = rot8[:, 5:7], rot8[:, 7]
        khl = sb("khl", [P, 2, 2, G * S], F16)
        qhl = sb("qhl", [P, 2, 2, G * S], F16)
        KA = sb("KA", [P, H, S], F16)
        QH = sb("QH", [P, H, S], F16)
        QL = sb("QL", [P, H, S], F16)
        mx3 = sb("mx3", [P, H, 3])
        MT = sb("MT", [P, S], F16)
        rcp = sb("rcp", [P, 2, S])

        PT = ctx.enter_context(nc.psum_tensor("PT", [P, 2, 1024], F32))
        PM = ctx.enter_context(nc.psum_tensor("PM", [P, 2, 512], F32))
        PO = ctx.enter_context(nc.psum_tensor("PO", [P, 2, 512], F32))

        loaded, w_loaded = sem("loaded"), sem("w_loaded")
        s_pool0, s_onehot = sem("constants_set"), sem("onehot_rows_set")
        s_wprod, s_wcopy = sem("weight_products"), sem("weight_products_kept")
        s_pe, s_act, s_dve, s_pool = sem("pe_done"), sem("act_done"), sem("dve_done"), sem("pool_done")
        chain = sem("dve_chain")
        pchain = sem("pool_chain")
        shuf_k, shuf_q, s_out = sem("keys_moved"), sem("queries_moved"), sem("stored")
        del s_pe, s_act, s_dve, s_pool
        PER = {}
        SEM = {}

        def ev(name, per):
            SEM[name] = sem(name)
            PER[name] = per
            return name

        ev("xeT_ready", 1); ev("kproj", 1); ev("qproj", 1); ev("vproj", 1)
        ev("k_high", 1); ev("q_high", 1); ev("heads_masked", 1); ev("q_split", 1); ev("v_kept", 1)
        ev("smax_scores", H); ev("smax_read", H); ev("nm_ready", 1); ev("nmT", 1); ev("nmT_kept", 1)
        ev("scores", 8); ev("probs", 8); ev("pv", 4); ev("pv_kept", 1); ev("sums", 1); ev("att_ready", 1)
        ev("wo_done", 1); ev("x1_ready", 1); ev("x1T", 1); ev("x1T_kept", 1)
        ev("logits", 1); ev("gate_shifted", 1); ev("gate_exp", 1)
        ev("h_up", E); ev("h_tanh", E); ev("h_ready", E); ev("y_done", E); ev("y_added", E)
        ev("x2_ready", 1); ev("x2T", 1); ev("x2T_kept", 1)
        ev("latp", 1); ev("lat_kept", 1); ev("qF", 1); ev("qS", 1); ev("kF", 1); ev("kS", 1)
        ev("k_raw", 2); ev("k_rot", 2); ev("k_hi", 2); ev("k_lo", 2)
        ev("q_rot", 2); ev("q_hi", 2); ev("q_lo", 2)
        ev("smax1", H); ev("smax1_read", H); ev("nm1_ready", 1); ev("nm1T", 1); ev("nm1T_kept", 1)
        ev("scores1", 8); ev("probs1", 8); ev("pv1", 8); ev("ol", 8)
        ev("wo1_done", 1); ev("x3_ready", 1); ev("x3T", 1); ev("x3T_kept", 1)
        ev("ffn", 1); ev("y_out", 1)

        def wait(eng, name, b, n=None):
            n = PER[name] if n is None else n
            eng.wait_ge(SEM[name], b * PER[name] + n)

        def sig(ins, name):
            ins.then_inc(SEM[name], 1)

        ident, i16 = c["ident"], c["i16"]
        block = ctx.enter_context(nc.Block())

        n_c = len(names) + 4
        w_src = [(kup, "w_kup"), (kvd, "w_kvd"), (vup, "w_vup"), (wo1, "w_o1"), (W1, "W1"), (W2T, "W2T"), (b1, "b1"), (b2, "b2")]

        @block.sync
        def _(sp):
            for dst, n in ((x_sb, "x"), (xT_sb, "xT"), (pe_sb, "pe"), (peT_sb, "peT")):
                sp.dma_start(dst[:], a[n]).then_inc(loaded, 16)
            for n in names:
                sp.dma_start(names[n][:], a[n]).then_inc(loaded, 16)
            for dst, n in w_src:
                sp.dma_start(dst if dst is W1 or dst is W2T or dst is kup or dst is wo1 else dst[:], a[n]).then_inc(w_loaded, 16)
            sp.wait_ge(loaded, 16 * n_c)
            with sp.Fori(0, B) as b:
                def move(dst, lo_row, src):
                    for j in range(4):
                        yield sp.dma_start(dst[lo_row:lo_row + 32, 4 * j:4 * j + 4, :],
                                           src[32 * j:32 * j + 32, :].rearrange("p (g n) -> p g n", g=G))
                for half in range(2):
                    wait(sp, "k_hi", b, half + 1)
                    for d in move(KA, 32 * half, khl[:, 0, half, :]):
                        d.then_inc(shuf_k, 16)
                    wait(sp, "q_hi", b, half + 1)
                    for rep in range(2):
                        for d in move(QH, 64 * rep + 32 * half, qhl[:, 0, half, :]):
                            d.then_inc(shuf_q, 16)
                for half in range(2):
                    wait(sp, "k_lo", b, half + 1)
                    for d in move(KA, 64 + 32 * half, khl[:, 1, half, :]):
                        d.then_inc(shuf_k, 16)
                    wait(sp, "q_lo", b, half + 1)
                    for rep in range(2):
                        for d in move(QL, 64 * rep + 32 * half, qhl[:, 1, half, :]):
                            d.then_inc(shuf_q, 16)

        @block.gpsimd
        def _(pool):
            nc.gpsimd.memset(V0[:], 0.0).then_inc(pchain, 1)
            nc.gpsimd.memset(nm[:], 0.0).then_inc(s_pool0, 1)
            nc.gpsimd.memset(MT[:], 0.0).then_inc(s_pool0, 1)
            nc.gpsimd.memset(gp[:], -1.0).then_inc(s_pool0, 1)
            nc.gpsimd.memset(ones64[:], 1.0).then_inc(s_pool0, 1)
            nc.gpsimd.memset(ones_row[:], 1.0).then_inc(s_pool0, 1)
            pool.wait_ge(pchain, 1)
            nc.gpsimd.memset(V0[:, :, :, HD0:HD0 + 1], 1.0).then_inc(s_pool0, 1)
            pool.wait_ge(loaded, 16 * n_c)
            PCH = 8
            with pool.Fori(0, B) as b:
                n = [0]

                def link(ins):
                    n[0] += 1
                    ins.then_inc(pchain, 1)
                    return n[0]

                def linked(k):
                    pool.wait_ge(pchain, b * PCH + k + 1)

                cosb = c["cos"][:].unsqueeze(1).to_broadcast([P, G, S])
                sinb = c["sin"][:].unsqueeze(1).to_broadcast([P, G, S])

                def v4(t):
                    return t.rearrange("p (g s) -> p g s", g=G)
                wait(pool, "k_raw", b)
                link(nc.gpsimd.tensor_tensor(v4(kr[:, 0]), v4(kraw[:, 0]), cosb, ALU.mult))
                linked(link(nc.gpsimd.tensor_tensor(v4(kt), v4(kraw[:, 1]), sinb, ALU.mult)))
                sig(nc.gpsimd.tensor_tensor(kr[:, 0], kr[:, 0], kt, ALU.subtract), "k_rot")
                link(nc.gpsimd.tensor_tensor(v4(kr[:, 1]), v4(kraw[:, 1]), cosb, ALU.mult))
                wait(pool, "k_rot", b, 1)
                linked(link(nc.gpsimd.tensor_tensor(v4(kt), v4(kraw[:, 0]), sinb, ALU.mult)))
                sig(nc.gpsimd.tensor_tensor(kr[:, 1], kr[:, 1], kt, ALU.add), "k_rot")
                for half in range(2):
                    wait(pool, "k_hi", b, half + 1)
                    wait(pool, "k_rot", b, half + 1)
                    sig(nc.gpsimd.tensor_tensor(khl[:, 1, half], kr[:, half], khl[:, 0, half], ALU.subtract), "k_lo")
                for _ in range(PCH - n[0]):
                    pool.sem_inc(pchain, 1)

        @block.scalar
        def _(act):
            for n, (dst, src) in enumerate([(wk_eff[:, 0], PT[:, 0, 0:512]), (wk_eff[:, 1], PT[:, 0, 512:1024])]
                                           + [(vo[:], PT[:, 1, :])]):
                act.wait_ge(s_wprod, n + 1)
                nc.scalar.copy(dst.rearrange("p g n -> p (g n)"), src).then_inc(s_wcopy, 1)
            for n in range(4):
                act.wait_ge(s_wprod, 4 + n)
                dst = (Wc, bc)[n // 2]
                bank = (PM, PO)[n // 2]
                nc.scalar.copy(dst[:, 4 * (n % 2):4 * (n % 2) + 4].rearrange("p g n -> p (g n)"),
                               bank[:, n % 2, :]).then_inc(s_wcopy, 1)
            act.wait_ge(loaded, 16 * n_c)
            with act.Fori(0, B) as b:
                wait(act, "kproj", b)
                for g in range(G):
                    ins = nc.scalar.activation(K4[:, g, :], PT[0:96, 0, g * S:(g + 1) * S], ACT.Identity,
                                               bias=c["bk"][0:96, g:g + 1])
                sig(ins, "k_high")
                wait(act, "qproj", b)
                for g in range(G):
                    ins = nc.scalar.activation(Q4[0:96, g, :], PT[0:96, 1, g * S:(g + 1) * S], ACT.Identity,
                                               bias=c["bq"][0:96, g:g + 1])
                sig(ins, "q_high")
                wait(act, "nmT", b)
                sig(nc.scalar.copy(Q4[96:P, :, :], PM[96:P, 0, 0:S].unsqueeze(1).to_broadcast([32, G, S])), "nmT_kept")
                for s in range(8):
                    wait(act, "scores", b, s + 1)
                    if s >= 4:
                        wait(act, "pv", b, (s - 4) // 2 + 1)
                    sig(nc.scalar.activation(Pr[:, s % 4, :], PT[:, s % 2, :], ACT.Exp, scale=SCALE0), "probs")
                wait(act, "pv", b)
                sig(nc.scalar.copy(U, PO[:].rearrange("p a n -> p (a n)")), "pv_kept")
                wait(act, "x1T", b)
                sig(nc.scalar.copy(xnT[:], PM[:, 0, 0:S]), "x1T_kept")
                wait(act, "gate_shifted", b)
                sig(nc.scalar.activation(ge[:], lg[:], ACT.Exp), "gate_exp")
                for e in range(E):
                    wait(act, "h_up", b, e + 1)
                    if e >= 2:
                        wait(act, "y_done", b, e - 1)
                    sig(nc.scalar.activation(th[:, e % 2, :], PT[:, e % 2, 512 * (e // 2 % 2):512 * (e // 2 % 2) + 512],
                                             ACT.Tanh, scale=0.5), "h_tanh")
                wait(act, "x2T", b)
                sig(nc.scalar.copy(xnT[:], PM[:, 0, 0:S]), "x2T_kept")
                wait(act, "latp", b)
                sig(nc.scalar.copy(lat[:].rearrange("p t l -> p (t l)"), PM[:, 0, 0:T * LAT]), "lat_kept")
                wait(act, "kF", b)
                sig(nc.scalar.copy(kraw[:, 0], PT[:, 0, :]), "k_raw")
                wait(act, "kS", b)
                sig(nc.scalar.copy(kraw[:, 1], PT[:, 1, :]), "k_raw")
                for half in range(2):
                    wait(act, "q_rot", b, half + 1)
                    sig(nc.scalar.copy(qhl[:, 0, half], qr[:, half]), "q_hi")
                    wait(act, "k_rot", b, half + 1)
                    sig(nc.scalar.copy(khl[:, 0, half], kr[:, half]), "k_hi")
                wait(act, "nm1T", b)
                sig(nc.scalar.copy(MT[0:32, :], PM[0:32, 0, 0:S]), "nm1T_kept")
                for s in range(8):
                    wait(act, "scores1", b, s + 1)
                    if s >= 4:
                        wait(act, "pv1", b, s - 3)
                    sig(nc.scalar.activation(Pr[:, s % 4, 0:768], PT[:, s % 2, 0:768], ACT.Exp, scale=SCALE1), "probs1")
                wait(act, "x3T", b)
                sig(nc.scalar.copy(xnT[:], PM[:, 0, 0:S]), "x3T_kept")
                wait(act, "y_out", b)
                act.dma_start(out[bass.ds(b, 1)].rearrange("a (t p) d -> p (a t) d", p=P), ln_t[:]).then_inc(s_out, 16)
                act.wait_ge(s_out, b * 16 + 16)

        @block.vector
        def _(dve):
            v = nc.vector
            dve.wait_ge(loaded, 16 * n_c)
            v.tensor_copy(Km[96:P, :, :, :].rearrange("p g j s -> p (g j) s"),
                          c["onehot0"][96:P, :].unsqueeze(2).to_broadcast([32, H, S])).then_inc(s_onehot, 1)
            dve.wait_ge(s_pool0, 6)
            dve.wait_ge(s_wcopy, 7)
            with dve.Fori(0, B) as b:
                n = [0]

                def link(ins):
                    n[0] += 1
                    ins.then_inc(chain, 1)
                    dve.wait_ge(chain, b * VCH + n[0])

                def held():
                    v.memset(spare[:], 0.0)

                def layer_norm(src, dst):
                    for t in range(T):
                        i = v.bn_stats(st[:, t], src[:, t])
                    link(i)
                    held()
                    for t in range(T):
                        i = v.bn_aggr(mv[:, t], st[:, t])
                    link(i)
                    link(v.tensor_scalar(wv[:], mv[:, :, 1], LN_EPS, None, ALU.add))
                    link(v.tensor_scalar(rs[:].bitcast(I32), wv[:].bitcast(I32), 1, None, ALU.arith_shift_right))
                    link(v.tensor_scalar(rs[:].bitcast(I32), rs[:].bitcast(I32), -1.0, RSQRT_BITS, ALU.mult, ALU.add))
                    for _ in range(3):
                        link(v.scalar_tensor_tensor(out=rw[:], in0=rs[:], scalar=-0.5, in1=rs[:], op0=ALU.mult, op1=ALU.mult))
                        link(v.tensor_tensor(rw[:], rw[:], wv[:], ALU.mult))
                        link(v.scalar_tensor_tensor(out=rs[:], in0=rw[:], scalar=1.5, in1=rs[:], op0=ALU.add, op1=ALU.mult))
                    for t in range(T):
                        i = v.tensor_scalar(dst[:, t], src[:, t], mv[:, t, 0:1], rs[:, t:t + 1],
                                            ALU.subtract, ALU.mult)
                    return i

                sig(v.tensor_tensor(xeT[:], xT_sb[:, bass.ds(b * S, S)], peT_sb[:], ALU.add), "xeT_ready")
                link(v.tensor_tensor(xb[:], x_sb[:, bass.ds(b * T, T), :], c["bo_b"][:].unsqueeze(1).to_broadcast([P, T, D]), ALU.add))
                v.tensor_tensor(xe[:], xb[:], pe_sb[:], ALU.add)
                wait(dve, "k_high", b)
                for g in range(G):
                    i = v.scalar_tensor_tensor(out=K4[32:64, g, :], in0=PT[32:64, 0, g * S:(g + 1) * S],
                                               scalar=c["bk"][32:64, g:g + 1], in1=K4[32:64, g, :],
                                               op0=ALU.add, op1=ALU.subtract)
                link(i)
                for j in range(4):
                    i = v.tensor_scalar(Km[0:96, :, j, :], K4[:], c["hmask"][0:96, j:j + 1], None, ALU.mult)
                sig(i, "heads_masked")
                wait(dve, "q_high", b)
                for g in range(G):
                    i = v.scalar_tensor_tensor(out=Q4[64:96, g, :], in0=PT[64:96, 1, g * S:(g + 1) * S],
                                               scalar=c["bq"][64:96, g:g + 1], in1=Q4[64:96, g, :],
                                               op0=ALU.add, op1=ALU.subtract)
                sig(i, "q_split")
                wait(dve, "vproj", b)
                sig(v.tensor_tensor(V0[:, :, :, 0:HD0], PO[:, 0, 0:T * D].rearrange("p (t h d) -> p t h d", t=T, d=HD0),
                                    c["bv_b"][:].rearrange("p (h d) -> p h d", d=HD0).unsqueeze(1).to_broadcast([P, T, H, HD0]),
                                    ALU.add), "v_kept")
                for h in range(H):
                    wait(dve, "smax_scores", b, h + 1)
                    i = v.reduce_max(mx[:, :, h], PM[:, h % 2, :].rearrange("p (t k) -> p t k", t=T), AX.X)
                    sig(i, "smax_read")
                wait(dve, "smax_read", b)
                sig(v.tensor_scalar(nm[:, :, 0:H], mx[:], -1.0, None, ALU.mult), "nm_ready")
                wait(dve, "sums", b)
                link(v.reciprocal(att[:], PM[:].rearrange("p a n -> p (a n)")))
                sig(v.tensor_tensor(att[:], att[:], U, ALU.mult), "att_ready")
                wait(dve, "wo_done", b)
                link(v.tensor_tensor(ln_s[:], PT[:, 0, 0:T * D].rearrange("p (t d) -> p t d", t=T), xe[:], ALU.add))
                link(layer_norm(ln_s, ln_t))
                link(v.tensor_tensor(ln_t[:], ln_t[:], c["gamma_b"][:].unsqueeze(1).to_broadcast([P, T, D]), ALU.mult))
                link(v.tensor_tensor(ln_t[:], ln_t[:], c["beta_b"][:].unsqueeze(1).to_broadcast([P, T, D]), ALU.add))
                link(v.tensor_tensor(ln_s[:], ln_t[:], x_sb[:, bass.ds(b * T, T), :], ALU.add))
                sig(layer_norm(ln_s, x1), "x1_ready")
                wait(dve, "logits", b)
                lgp = PM[:, 1, 0:T * E].rearrange("p (t e) -> p t e", t=T)
                link(v.reduce_max(lmx[:], lgp, AX.X))
                sig(v.tensor_tensor(lg[:], lgp, lmx[:].unsqueeze(2).to_broadcast([P, T, E]), ALU.subtract), "gate_shifted")
                wait(dve, "gate_exp", b)
                link(v.reduce_sum(gs[:], ge[:], AX.X))
                link(v.reciprocal(gs[:], gs[:]))
                link(v.tensor_tensor(gp[:, :, 0:E], ge[:], gs[:].unsqueeze(2).to_broadcast([P, T, E]), ALU.mult))
                held()
                for t in range(T):
                    i = v.max(top[:, t], gp[:, t, 0:E])
                link(i)
                link(v.memset(top[:, :, 2:8], -1.0))
                held()
                for t in range(T):
                    i = v.match_replace(gr[:, t], top[:, t], gp[:, t], -2.0)
                link(i)
                link(v.tensor_tensor(gr[:, :, 0:E], gr[:, :, 0:E], gp[:, :, 0:E], ALU.not_equal))
                link(v.tensor_tensor(cw[:], gr[:, :, 0:E], gp[:, :, 0:E], ALU.mult))
                link(v.reduce_sum(gs[:], cw[:], AX.X))
                link(v.tensor_scalar(gs[:], gs[:], GATE_EPS, None, ALU.max))
                link(v.reciprocal(gs[:], gs[:]))
                link(v.tensor_tensor(cw[:], cw[:], gs[:].unsqueeze(2).to_broadcast([P, T, E]), ALU.mult))
                link(v.tensor_scalar(cw[:], cw[:], 0.5, None, ALU.mult))

                def up(e):
                    wait(dve, "h_tanh", b, e + 1)
                    sig(v.scalar_tensor_tensor(out=hT[:, e % 2].rearrange("p c s -> p (c s)"), in0=th[:, e % 2, :], scalar=1.0,
                                               in1=PT[:, e % 2, 512 * (e // 2 % 2):512 * (e // 2 % 2) + 512],
                                               op0=ALU.add, op1=ALU.mult), "h_ready")

                def down(e):
                    wait(dve, "y_done", b, e + 1)
                    if e:
                        wait(dve, "y_added", b, e)
                    for t in range(T):
                        i = v.scalar_tensor_tensor(out=y[:, (e + 1) % 2, t], in0=PO[:, e % 2, t * D:(t + 1) * D],
                                                   scalar=cw[:, t, e:e + 1],
                                                   in1=(y[:, e % 2, t] if e else x1[:, t]),
                                                   op0=ALU.mult, op1=ALU.add)
                    sig(i, "y_added")

                up(0)
                for e in range(1, E):
                    up(e)
                    down(e - 1)
                down(E - 1)
                wait(dve, "y_added", b)
                sig(layer_norm(y[:, E % 2], x1), "x2_ready")
                cosb = c["cos"][:].unsqueeze(1).to_broadcast([P, G, S])
                sinb = c["sin"][:].unsqueeze(1).to_broadcast([P, G, S])
                qp = [t.rearrange("p a (g s) -> p (a g) s", s=S) for t in (PM[:], PO[:])]

                def v4(t):
                    return t.rearrange("p (g s) -> p g s", g=G)
                wait(dve, "qF", b)
                v.tensor_tensor(v4(qr[:, 0]), qp[0], cosb, ALU.mult)
                wait(dve, "qS", b)
                link(v.tensor_tensor(v4(qt), qp[1], sinb, ALU.mult))
                sig(v.tensor_tensor(qr[:, 0], qr[:, 0], qt, ALU.subtract), "q_rot")
                v.tensor_tensor(v4(qr[:, 1]), qp[1], cosb, ALU.mult)
                wait(dve, "q_rot", b, 1)
                link(v.tensor_tensor(v4(qt), qp[0], sinb, ALU.mult))
                sig(v.tensor_tensor(qr[:, 1], qr[:, 1], qt, ALU.add), "q_rot")
                for half in range(2):
                    wait(dve, "q_hi", b, half + 1)
                    wait(dve, "q_rot", b, half + 1)
                    sig(v.tensor_tensor(qhl[:, 1, half], qr[:, half], qhl[:, 0, half], ALU.subtract), "q_lo")
                for h in range(H):
                    wait(dve, "smax1", b, h + 1)
                    sig(v.reduce_max(mx3[:, h, :], PM[:, h % 2, 0:384].rearrange("p (t k) -> p t k", t=3), AX.X), "smax1_read")
                wait(dve, "smax1_read", b)
                link(v.tensor_tensor(mx[:, 1, :], mx3[:, :, 1], mx3[:, :, 2], ALU.max))
                v.tensor_scalar(nm[:, 0, 0:H], mx3[:, :, 0], -1.0, None, ALU.mult)
                sig(v.tensor_scalar(nm[:, 1, 0:H], mx[:, 1, :], -1.0, None, ALU.mult), "nm1_ready")
                for s in range(8):
                    wait(dve, "pv1", b, s + 1)
                    link(v.reciprocal(rcp[:, s % 2], PO[:, s % 2, 256:512]))
                    sig(v.tensor_tensor(OL[:, s], PO[:, s % 2, 0:256], rcp[:, s % 2], ALU.mult), "ol")
                wait(dve, "wo1_done", b)
                link(v.tensor_tensor(ln_s[:], PT[:, 0, 0:T * D].rearrange("p (t d) -> p t d", t=T), x1[:], ALU.add))
                sig(layer_norm(ln_s, x1), "x3_ready")
                wait(dve, "ffn", b)
                wait(dve, "x3_ready", b)
                link(v.tensor_tensor(ln_s[:], PT[:, 0, 0:T * D].rearrange("p (t d) -> p t d", t=T), x1[:], ALU.add))
                link(v.tensor_tensor(ln_s[:], ln_s[:], bc[:, bass.ds(b, 1), :].to_broadcast([P, T, D]), ALU.add))
                sig(layer_norm(ln_s, ln_t), "y_out")
                dve.wait_ge(s_out, b * 16 + 16)
                assert n[0] <= VCH, n[0]
                for _ in range(VCH - n[0]):
                    dve.sem_inc(chain, 1)

        @block.tensor
        def _(pe):
            mm = nc.tensor.matmul
            pe.wait_ge(w_loaded, 16 * len(w_src))
            pe.wait_ge(s_pool0, 6)
            pe.wait_ge(s_onehot, 1)
            for f in range(2):
                for j in range(1):
                    mm(PT[:, 0, 512 * f:512 * f + 512], kvd[:], kup[:, 512 * f:512 * f + 512], start=True, stop=True).then_inc(s_wprod, 1)
            for p in range(H // 2):
                for hh in range(2):
                    r = slice(64 * hh, 64 * hh + 64)
                    i = mm(PT[r, 1, p * D:(p + 1) * D], vup[r, p, :], wo1[r, p, :], start=True, stop=True)
            i.then_inc(s_wprod, 1)
            for q in range(2):
                for g in range(4 * q, 4 * q + 4):
                    for o in range(OCH):
                        i = mm(PM[:, q, (g % 4) * D:(g % 4 + 1) * D], W1[:, g * OCH + o, :], W2T[:, g * OCH + o, :],
                               start=o == 0, stop=o == OCH - 1)
                i.then_inc(s_wprod, 1)
            for q in range(2):
                for g in range(4 * q, 4 * q + 4):
                    for o in range(OCH):
                        mm(PO[:, q, (g % 4) * D:(g % 4 + 1) * D], b1[:, g * OCH + o:g * OCH + o + 1].to_broadcast([P, P]),
                           W2T[:, g * OCH + o, :], start=o == 0, stop=False)
                    i = mm(PO[:, q, (g % 4) * D:(g % 4 + 1) * D], ones_row[0:1, :], b2[0:1, g * D:(g + 1) * D], start=False, stop=True)
                i.then_inc(s_wprod, 1)
            pe.wait_ge(loaded, 16 * n_c)
            pe.wait_ge(s_wcopy, 7)
            with pe.Fori(0, B) as b:
                wait(pe, "xeT_ready", b)
                for g in range(G):
                    i = mm(PT[0:96, 0, g * S:(g + 1) * S], c["wk3"][:, g, :], xeT[:], start=True, stop=True)
                sig(i, "kproj")
                for g in range(G):
                    i = mm(PT[0:96, 1, g * S:(g + 1) * S], c["wq3"][:, g, :], xeT[:], start=True, stop=True)
                sig(i, "qproj")
                for t in range(T):
                    i = mm(PO[:, 0, t * D:(t + 1) * D], xeT[:, t * P:(t + 1) * P], c["wv0"][:], start=True, stop=True)
                sig(i, "vproj")
                wait(pe, "heads_masked", b)
                wait(pe, "q_split", b)
                for h in range(H):
                    if h >= 2:
                        wait(pe, "smax_read", b, h - 1)
                    for t in range(T):
                        i = mm(PM[:, h % 2, t * S:(t + 1) * S], Q4[0:96, h // 4, t * P:(t + 1) * P], Km[0:96, h // 4, h % 4, :],
                               start=True, stop=True)
                    sig(i, "smax_scores")
                wait(pe, "nm_ready", b)
                for t in range(T):
                    i = mm(PM[96:P, 0, t * P:(t + 1) * P], nm[:, t, :], i16[:], start=True, stop=True, tile_position=(0, 96))
                sig(i, "nmT")
                wait(pe, "nmT_kept", b)
                wait(pe, "v_kept", b)

                def scores(s):
                    if s >= 2:
                        wait(pe, "probs", b, s - 1)
                    for hh in range(2):
                        h = 2 * s + hh
                        for k in range(T):
                            i = mm(PT[:, s % 2, (hh * 2 + k) * S:(hh * 2 + k + 1) * S],
                                   Km[:, h // 4, h % 4, k * P:(k + 1) * P], Q4[:, h // 4, :], start=True, stop=True)
                    sig(i, "scores")

                def values(g):
                    wait(pe, "probs", b, 2 * g + 2)
                    for k in range(T):
                        for j in range(4):
                            s, hh = 2 * g + j // 2, j % 2
                            i = mm(PO[32 * j:32 * j + 32, g // 2, (g % 2) * S:(g % 2 + 1) * S], V0[:, k, 4 * g + j, :],
                                   Pr[:, s % 4, (hh * 2 + k) * S:(hh * 2 + k + 1) * S], start=k == 0, stop=k == 1,
                                   tile_position=(0, 32 * j))
                    sig(i, "pv")

                for s in range(8):
                    scores(s)
                    if s >= 2 and s % 2 == 0:
                        values(s // 2 - 1)
                values(3)
                wait(pe, "pv_kept", b)
                for q in range(2):
                    i = mm(PM[:, q, :], c["sumsel"][:], U[:, q * 512:(q + 1) * 512], start=True, stop=True)
                sig(i, "sums")
                wait(pe, "att_ready", b)
                for t in range(T):
                    for g in range(G):
                        i = mm(PT[:, 0, t * D:(t + 1) * D], att[:, g * S + t * P:g * S + (t + 1) * P], c["wo0"][:, g, :],
                               start=g == 0, stop=g == G - 1)
                sig(i, "wo_done")
                wait(pe, "x1_ready", b)
                for t in range(T):
                    i = nc.tensor.transpose(PM[:, 0, t * P:(t + 1) * P], x1[:, t], ident[:])
                sig(i, "x1T")
                wait(pe, "x1T_kept", b)
                for t in range(T):
                    i = mm(PM[:, 1, t * E:(t + 1) * E], xnT[:, t * P:(t + 1) * P], c["router"][:], start=True, stop=True)
                sig(i, "logits")

                def up(e):
                    if e >= 4:
                        wait(pe, "h_ready", b, e - 3)
                    for f in range(2):
                        i = mm(PT[:, e % 2, 512 * (e // 2 % 2) + f * S:512 * (e // 2 % 2) + (f + 1) * S],
                               c["w1"][:, e, f * P:(f + 1) * P], xnT[:], start=True, stop=True)
                    sig(i, "h_up")

                def down(e):
                    wait(pe, "h_ready", b, e + 1)
                    if e >= 2:
                        wait(pe, "y_added", b, e - 1)
                    for t in range(T):
                        for f in range(2):
                            i = mm(PO[:, e % 2, t * D:(t + 1) * D], hT[:, e % 2, f, t * P:(t + 1) * P], c["w2"][:, e, f, :],
                                   start=f == 0, stop=f == 1)
                    sig(i, "y_done")

                up(0)
                for e in range(1, E):
                    up(e)
                    down(e - 1)
                down(E - 1)
                wait(pe, "x2_ready", b)
                for t in range(T):
                    i = nc.tensor.transpose(PM[:, 0, t * P:(t + 1) * P], x1[:, t], ident[:])
                sig(i, "x2T")
                wait(pe, "x2T_kept", b)
                for name, w, dst, half in (("kF", wk_eff, PT[:, 0], 0), ("kS", wk_eff, PT[:, 1], 1),
                                           ("latp", None, None, 0),
                                           ("qS", c["wq1"], PO[:].rearrange("p a n -> p (a n)"), 1),
                                           ("qF", c["wq1"], PM[:].rearrange("p a n -> p (a n)"), 0)):
                    if name == "latp":
                        for t in range(T):
                            i = mm(PM[:, 0, t * LAT:(t + 1) * LAT], xnT[:, t * P:(t + 1) * P], c["wkvT"][:], start=True, stop=True)
                    else:
                        if name == "qF":
                            wait(pe, "lat_kept", b)
                        for g in range(G):
                            i = mm(dst[:, g * S:(g + 1) * S], w[:, half, g, :], xnT[:], start=True, stop=True)
                    sig(i, name)
                pe.wait_ge(shuf_k, b * 256 + 256)
                pe.wait_ge(shuf_q, b * 512 + 512)
                for h in range(H):
                    if h >= 2:
                        wait(pe, "smax1_read", b, h - 1)
                    for t in range(T):
                        q, k, o = slice(t * P, (t + 1) * P), slice(0, (t + 1) * P), t * P
                        region = PM[:, h % 2, o:o + (t + 1) * P]
                        mm(region, QH[:, h, q], KA[:, h, k], start=True, stop=False)
                        mm(region, QL[:, h, q], KA[:, h, k], start=False, stop=False)
                        i = mm(PM[:, h % 2, o + t * P:o + (t + 1) * P], i16[:], c["future_k"][:], start=False, stop=True)
                    sig(i, "smax1")
                wait(pe, "nm1_ready", b)
                for t in range(T):
                    i = mm(PM[0:32, 0, t * P:(t + 1) * P], nm[:, t, :], i16[:], start=True, stop=True)
                sig(i, "nm1T")
                wait(pe, "nm1T_kept", b)

                def scores1(s):
                    if s >= 2:
                        wait(pe, "probs1", b, s - 1)
                    for k in range(T):
                        for hh in range(2):
                            h = 2 * s + hh
                            q = slice(k * P, S)
                            o = hh * S if k == 0 else 2 * S + hh * P
                            n = S - k * P
                            region = PT[:, s % 2, o:o + n]
                            mm(region, KA[:, h, k * P:(k + 1) * P], QH[:, h, q], start=True, stop=False)
                            mm(region, KA[:, h, k * P:(k + 1) * P], QL[:, h, q], start=False, stop=False)
                            mm(region, i16[:, h:h + 1].to_broadcast([P, P]), MT[:, q], start=False, stop=False)
                            i = mm(PT[:, s % 2, o:o + P], i16[:], c["future_q"][:], start=False, stop=True)
                    sig(i, "scores1")

                def values1(s):
                    wait(pe, "probs1", b, s + 1)
                    if s >= 2:
                        wait(pe, "ol", b, s - 1)
                    for col, stat in ((0, [lat[:, 0], lat[:, 1]]), (S, [ones64[:], ones64[:]])):
                        for k in range(T):
                            for hh in range(2):
                                o = hh * S if k == 0 else 2 * S + hh * P
                                i = mm(PO[64 * hh:64 * hh + 64, s % 2, col + k * P:col + S], stat[k],
                                       Pr[:, s % 4, o:o + S - k * P], start=k == 0, stop=k == 1, tile_position=(0, 64 * hh))
                    sig(i, "pv1")

                for s in range(8):
                    scores1(s)
                    if s:
                        values1(s - 1)
                values1(7)
                wait(pe, "ol", b)
                for t in range(T):
                    for p in range(H // 2):
                        i = mm(PT[:, 0, t * D:(t + 1) * D], OL[:, p, t * P:(t + 1) * P], vo[:, p, :],
                               start=p == 0, stop=p == H // 2 - 1)
                sig(i, "wo1_done")
                wait(pe, "x3_ready", b)
                for t in range(T):
                    i = nc.tensor.transpose(PM[:, 0, t * P:(t + 1) * P], x1[:, t], ident[:])
                sig(i, "x3T")
                wait(pe, "x3T_kept", b)
                for t in range(T):
                    i = mm(PT[:, 0, t * D:(t + 1) * D], xnT[:, t * P:(t + 1) * P],
                           Wc[:, bass.ds(b, 1), :].rearrange("p a n -> p (a n)"), start=True, stop=True)
                sig(i, "ffn")


def layouts(i):
    f = np.float32
    asc = np.ascontiguousarray
    r = {}
    x = i["L0_attn_x"]
    r["x"] = asc(x.reshape(B * T, P, D).transpose(1, 0, 2))
    r["xT"] = asc(x.reshape(B * S, D).T)
    pe = i["L0_attn_pe"][0, :S]
    r["pe"] = asc(pe.reshape(T, P, D).transpose(1, 0, 2))
    r["peT"] = asc(pe.T)

    def thrice(w):
        w = w.reshape(-1, G, 32)
        return asc(np.concatenate([w, w, w], axis=2))
    r["wq3"], r["wk3"] = thrice(i["L0_attn_wq"]), thrice(i["L0_attn_wk"])
    r["bq"] = asc(thrice(i["L0_attn_bq"][None])[0].T)
    r["bk"] = asc(thrice(i["L0_attn_bk"][None])[0].T)
    r["wv0"] = i["L0_attn_wv"]
    wo = np.zeros((4, 32, G, D), f)
    wo[:, :HD0] = i["L0_attn_wo"].reshape(G, 4, HD0, D).transpose(1, 2, 0, 3)
    r["wo0"] = wo.reshape(P, G, D)
    for n, k in (("bv_b", "L0_attn_bv"), ("bo_b", "L0_attn_bo"), ("gamma_b", "L0_attn_gamma"), ("beta_b", "L0_attn_beta")):
        r[n] = asc(np.broadcast_to(i[k][None], (P, D)))
    r["router"] = i["L0_ffn_router_w"]
    r["w1"] = asc(i["L0_ffn_w1"].transpose(1, 0, 2))
    r["w2"] = asc(i["L0_ffn_w2"].reshape(E, 2, P, D).transpose(2, 0, 1, 3))

    def halves(w):
        w = w.reshape(4, G, 2, 32, -1)
        return asc(w.transpose(4, 2, 1, 0, 3))
    r["wq1"] = halves(i["L1_attn_wq"]).reshape(D, 2, G, P)
    r["w_kup"] = halves(i["L1_attn_w_k_up"]).reshape(LAT, H * HD1)
    r["w_kvd"] = i["L1_attn_w_kv_down"]
    r["wkvT"] = asc(i["L1_attn_w_kv_down"].T)
    r["w_vup"] = asc(i["L1_attn_w_v_up"].reshape(H // 2, P, LAT).transpose(1, 0, 2))
    r["w_o1"] = asc(i["L1_attn_wo"].T.reshape(H // 2, P, D).transpose(1, 0, 2))
    r["W1"] = asc(i["L1_ffn_W1"].reshape(B, OCH, P, D).transpose(2, 0, 1, 3).reshape(P, B * OCH, D))
    r["W2T"] = asc(i["L1_ffn_W2"].reshape(B, D, OCH, P).transpose(3, 0, 2, 1).reshape(P, B * OCH, D))
    r["b1"] = asc(i["L1_ffn_b1"].reshape(B, OCH, P).transpose(2, 0, 1).reshape(P, B * OCH))
    r["b2"] = asc(i["L1_ffn_b2"].reshape(1, B * D))

    r["ident"] = np.eye(P, dtype=f)
    r["i16"] = np.eye(P, dtype=np.float16)
    hmask = np.zeros((P, 4), f)
    for j in range(4):
        for q in range(3):
            hmask[32 * q + 8 * j:32 * q + 8 * j + 8, j] = 1
    r["hmask"] = hmask
    one = np.zeros((P, H), np.float16)
    one[96 + np.arange(H), np.arange(H)] = 1
    r["onehot0"] = one
    sel = np.zeros((4, 32, 4, 32), f)
    for j in range(4):
        sel[j, HD0, j] = 1
    r["sumsel"] = sel.reshape(P, P)
    q, k = np.indices((P, P))
    r["future_k"] = np.where(k > q, MASKED, 0).astype(np.float16)
    r["future_q"] = asc(r["future_k"].T)
    inv = (f(1.0) / (f(10000.0) ** (np.arange(0, HD1, 2, dtype=f) / f(HD1)))).astype(f)
    ang = (np.arange(S, dtype=f)[None] * inv[:, None]).astype(f)
    r["cos"] = asc(np.tile(np.cos(ang), (4, 1)))
    r["sin"] = asc(np.tile(np.sin(ang), (4, 1)))
    return r


def program(nc, arrays):
    args = {n: nc.dram_tensor(f"in_{n}", v.shape, mybir.dt.from_np(v.dtype), kind="ExternalInput").ap() for n, v in arrays.items()}
    out = nc.dram_tensor("out_0", (B, S, D), F32, kind="ExternalOutput").ap()
    build(nc, args, out)


def kernel(**inputs):
    import concourse.bacc as _bacc
    from concourse.bass_utils import run_bass_kernel_spmd as _run

    arrays = layouts({k: np.asarray(v) for k, v in inputs.items()})
    nc = _bacc.Bacc("TRN2", target_bir_lowering=False, num_devices=1)
    program(nc, arrays)
    r = _run(nc, [{f"in_{n}": v for n, v in arrays.items()}], core_ids=[0])
    return r.results[0]["out_0"]
```

```python
from contextlib import ExitStack

import numpy as np

import concourse.bass as bass
from concourse import mybir

F32 = mybir.dt.float32
F16 = mybir.dt.float16
I32 = mybir.dt.int32
ALU = mybir.AluOpType
ACT = mybir.ActivationFunctionType
AX = mybir.AxisListType

B, S, D = 8, 256, 128
P = 128
T = S // P
H = 16
HD0, HD1 = 8, 64
G = H // 4
E, FI = 8, 256
LAT = 64
OCH = 4
LN_EPS, GATE_EPS = 1e-5, 1e-9
SCALE0, SCALE1 = HD0 ** -0.5, HD1 ** -0.5
RSQRT_BITS = float(0x5F3759DF)
DVE1, DVE2, DVE3, POOL2 = 34, 34, 32, 6
MASKED = -60000.0


def together(*parts):
    heads = [[next(p, None), n, p] for n, p in enumerate(parts)]
    while heads := [h for h in heads if h[0] is not None]:
        first = min(heads, key=lambda h: (h[0], h[1]))
        place = next(first[2], None)
        assert place is None or place >= first[0], (place, first[0])
        first[0] = place


def build(nc, a, out):
    ctx = ExitStack()
    with ctx:
        def sb(name, shape, dt=F32):
            return ctx.enter_context(nc.sbuf_tensor(name, shape, dt))

        def ps(name, shape):
            return ctx.enter_context(nc.psum_tensor(name, shape, F32))

        def sem(name):
            return ctx.enter_context(nc.semaphore(name))

        x_sb = sb("x_sb", [P, B * T, D])
        pe_sb = sb("pe_sb", [P, T, D])
        once = ("w_kup", "w_vup", "w_o1", "w_kvd", "W1", "W2T", "b1", "b2")
        c = {n: sb("c_" + n, list(v.shape), v.dtype) for n, v in a.items()
             if n not in ("x", "pe") + once}
        ident, i16 = c["ident"], c["i16"]
        wk_eff = sb("wk_eff", [P, 2, G, P])
        vo = sb("vo", [P, H // 2, D])
        Wc = sb("Wc", [P, B, D])
        bc = sb("bc", [P, B, D])

        xeT = sb("xeT", [P, S])
        xe = sb("xe", [P, T, D])
        K4 = sb("K4", [96, G, S], F16)
        Q4 = sb("Q4", [P, G, S], F16)
        Km = sb("Km", [P, G, 4, S], F16)
        V0 = sb("V0", [P, T, H, 32])
        mx = sb("mx", [P, T, H])
        nm = sb("nm", [P, T, 32], F16)
        Pr = sb("Pr", [P, 8, 512])
        U = sb("U", [P, G * S])
        rsum = sb("rsum", [P, S])
        x1 = sb("x1", [P, T, D])
        x1T = sb("x1T", [P, S])
        x2T = sb("x2T", [P, S])
        lg = sb("lg", [P, T, 8])
        lmx = sb("lmx", [P, T])
        ge = sb("ge", [P, T, 8])
        gp = sb("gp", [P, T, 16])
        top = sb("top", [P, T, 8])
        gr = sb("gr", [P, T, 16])
        gs = sb("gs", [P, T])
        cw = sb("cw", [P, T, 8])
        hT = sb("hT", [P, 2, 2, S])
        th = hT[:].rearrange("p e c s -> p e (c s)")
        y = sb("y", [P, 2, T, D])
        x2 = sb("x2", [P, T, D])
        lat = sb("lat", [P, T, LAT])
        C2 = G * S // 2
        raw = sb("raw", [P, 2, 2, C2])
        rot = sb("rot", [P, 2, 2, 2, C2])
        rtm = sb("rtm", [P, 2, C2])
        khl = sb("khl", [P, 2, 2, 2, C2], F16)
        qhl = sb("qhl", [P, 2, 2, 2, C2], F16)
        KQ = sb("KQ", [P, 3, H, S], F16)
        KA = KQ[:, 0]
        QH = KQ[:, 1]
        QL = KQ[:, 2]
        x2r = sb("x2r", [P, T, D])
        lat3 = sb("lat3", [P, T, LAT])
        mx3 = sb("mx3", [P, H, 3])
        nm3 = sb("nm3", [P, T, 32], F16)
        MT = sb("MT", [P, S], F16)
        Pr3 = sb("Pr3", [P, 4, 384])
        OL = sb("OL", [P, (H // 2 + 1) * S])
        ssum = sb("ssum", [P, S])
        x3 = sb("x3", [P, T, D])
        x3T = sb("x3T", [P, S])
        ln = {n: {k: sb(f"{k}{n}", sh) for k, sh in (("s", [P, T, D]), ("t", [P, T, D]), ("st", [P, T, 6]), ("mv", [P, T, 2]),
                                                    ("w", [P, T]), ("r", [P, T]), ("u", [P, T]))} for n in (1, 2, 3)}
        spare, pspare = sb("spare", [P, 1]), sb("pspare", [P, 2])
        W1 = KQ[:, 0:2].bitcast(F32).rearrange("p a h (o n) -> p (a h o) n", n=D)
        W2T = rot[:].rearrange("p a b e (o n) -> p (a b e o) n", n=D)
        kup = OL[0:LAT, 0:H * HD1]
        wo1 = OL[:, 1024:2048].rearrange("p (h n) -> p h n", n=D)
        kvd = OL[0:LAT, 2048:2048 + D]
        vup = raw[:, 0, 0].rearrange("p (h n) -> p h n", n=LAT)
        b1 = raw[:, 0, 1, 0:B * OCH]
        b2 = Pr3[0:1].rearrange("p a n -> p (a n)")[:, 0:B * D]
        ones_row = sb("ones_row", [1, P])

        PA, PAo = ps("PA", [P, 2, 512]), ps("PAo", [P, 512])
        PB = ps("PB", [P, 2, 512])
        PC, PCo = ps("PC", [P, 2, 512]), ps("PCo", [P, 512])

        loaded, w_loaded = sem("loaded"), sem("w_loaded")
        s_const, s_onehot = sem("constants_set"), sem("onehot_rows_set")
        s_wprod, s_wcopy = sem("weight_products"), sem("weight_products_kept")
        keys_moved, queries_moved, stored = sem("keys_moved"), sem("queries_moved"), sem("stored")

        def upto(b, per_row, n=None):
            return b * per_row + (per_row if n is None else n)

        def later(b):
            return not (isinstance(b, int) and b == 0)

        xe_ready, xe_done, xeT_ready, kproj, qproj = sem("xe_ready"), sem("xe_done"), sem("xeT_ready"), sem("kproj"), sem("qproj")
        vproj, k_high, q_high, k_low, heads_masked = sem("vproj"), sem("k_high"), sem("q_high"), sem("k_low"), sem("heads_masked")
        q_split, v_kept = sem("q_split"), sem("v_kept")
        smax, smax_read, nm_ready, nmT, nmT_kept = sem("smax"), sem("smax_read"), sem("nm_ready"), sem("nmT"), sem("nmT_kept")
        scores, probs, pv, pv_kept = sem("scores"), sem("probs"), sem("pv"), sem("pv_kept")
        sums, rsum_ready, sums_back, att_ready, wo_done = sem("sums"), sem("rsum_ready"), sem("sums_back"), sem("att_ready"), sem("wo_done")
        x1_ready, dve1 = sem("x1_ready"), sem("dve1")
        x1T_done, x1T_kept, logits, gate_shifted, gate_exp = sem("x1T_done"), sem("x1T_kept"), sem("logits"), sem("gate_shifted"), sem("gate_exp")
        h_up, h_tanh, h_ready, y_done, y_added = sem("h_up"), sem("h_tanh"), sem("h_ready"), sem("y_done"), sem("y_added")
        x2_ready, x2T_done, x2T_kept, latp, lat_kept = sem("x2_ready"), sem("x2T_done"), sem("x2T_kept"), sem("latp"), sem("lat_kept")
        proj, raw_kept, k_rot, k_hi, k_lo = sem("proj"), sem("raw_kept"), sem("k_rot"), sem("k_hi"), sem("k_lo")
        q_rot, q_hi, q_lo, dve2, pool2 = sem("q_rot"), sem("q_hi"), sem("q_lo"), sem("dve2"), sem("pool2")
        x2_kept, lat3_kept, smax3, smax3_read, nm3_ready = sem("x2_kept"), sem("lat3_kept"), sem("smax3"), sem("smax3_read"), sem("nm3_ready")
        nm3T, nm3T_kept, scores3, probs3 = sem("nm3T"), sem("nm3T_kept"), sem("scores3"), sem("probs3")
        pv3, pv3_kept, sums3_added, rsum3_ready, sums3_back = sem("pv3"), sem("pv3_kept"), sem("sums3_added"), sem("rsum3_ready"), sem("sums3_back")
        ol_ready = sem("ol_ready")
        wo1_done, x3_ready, x3T_done, x3T_kept, ffn = sem("wo1_done"), sem("x3_ready"), sem("x3T_done"), sem("x3T_kept"), sem("ffn")
        y_ready, dve3 = sem("y_ready"), sem("dve3")

        def rounds(eng, chain1, chain2, chain3):
            together(chain1(0))
            together(chain1(1), chain2(0))
            with eng.Fori(2, B) as r:
                together(chain1(r), chain2(r - 1), chain3(r - 2))
            together(chain2(B - 1), chain3(B - 2))
            together(chain3(B - 1))

        def at_smax(h):
            return 8 + 1.6 * h

        def at_scores(h):
            return 38 + 1.4 * h

        def at_expert(e):
            return 4 + 4 * e

        def at_proj(n):
            return (46, 48, 57, 59)[n]

        def at_turn(z, n):
            return (48, 50, 52, 59, 61, 63, 67, 69)[n] + 2 * z

        def at_smax3(h):
            return 1 + 1.6 * h

        def at_scores3(h):
            return 30 + 2 * h

        block = ctx.enter_context(nc.Block())
        n_c = len(c) + 2
        w_src = [(kup, "w_kup"), (kvd, "w_kvd"), (vup, "w_vup"), (wo1, "w_o1"), (W1, "W1"), (W2T, "W2T"), (b1, "b1"), (b2, "b2")]

        @block.sync
        def _(sp):
            for dst, n in w_src:
                sp.dma_start(dst, a[n]).then_inc(w_loaded, 16)
            for dst, n in ((x_sb, "x"), (pe_sb, "pe")):
                sp.dma_start(dst[:], a[n]).then_inc(loaded, 16)
            for n in c:
                sp.dma_start(c[n][:], a[n]).then_inc(loaded, 16)
            sp.wait_ge(loaded, 16 * n_c)

            def move_heads(b, first):
                def move(dst, row, src):
                    for j in range(4):
                        yield sp.dma_start(dst[row:row + 32, 4 * j:4 * j + 4, :].rearrange("p (a g) n -> p a (g n)", a=2),
                                           src[32 * j:32 * j + 32])
                if not first:
                    sp.wait_ge(scores3, upto(b - 1, H))
                sp.wait_ge(k_hi, upto(b, 2))
                for half in range(2):
                    for d in move(KA, 32 * half, khl[:, 0, :, half, :]):
                        d.then_inc(keys_moved, 16)
                sp.wait_ge(k_lo, upto(b, 2))
                for half in range(2):
                    for d in move(KA, 64 + 32 * half, khl[:, 1, :, half, :]):
                        d.then_inc(keys_moved, 16)
                for split, dst, part in ((q_hi, QH, 0), (q_lo, QL, 1)):
                    sp.wait_ge(split, upto(b, 2))
                    for half in range(2):
                        for rep in range(2):
                            for d in move(dst, 64 * rep + 32 * half, qhl[:, part, :, half, :]):
                                d.then_inc(queries_moved, 16)

            move_heads(0, True)
            with sp.Fori(1, B) as b:
                move_heads(b, False)

        def rotation(eng, engine, z, rotated, hi, lo, hl, b, link):
            cosb = c["cos"][:].unsqueeze(1).to_broadcast([P, 2, S])
            sinb = c["sin"][:].unsqueeze(1).to_broadcast([P, 2, S])
            t = rtm[:, z].rearrange("p (g s) -> p g s", s=S)
            for ch in range(2):
                first, second = (raw[:, z, i].rearrange("p (g s) -> p g s", s=S) for i in range(2))
                out1, out2 = (rot[:, z, ch, i].rearrange("p (g s) -> p g s", s=S) for i in range(2))
                yield at_turn(z, 3 * ch)
                engine.wait_ge(raw_kept, upto(b, 4, 2 * ch + z + 1))
                eng.tensor_tensor(out1, first, cosb, ALU.mult)
                link(eng.tensor_tensor(t, second, sinb, ALU.mult))
                yield at_turn(z, 3 * ch + 1)
                link(eng.tensor_tensor(out1, out1, t, ALU.subtract))
                eng.tensor_tensor(out2, second, cosb, ALU.mult)
                yield at_turn(z, 3 * ch + 2)
                link(eng.tensor_tensor(t, first, sinb, ALU.mult))
                eng.tensor_tensor(out2, out2, t, ALU.add).then_inc(rotated, 1)
            for ch in range(2):
                yield at_turn(z, 6 + ch)
                engine.wait_ge(hi, upto(b, 2, ch + 1))
                eng.tensor_tensor(hl[:, 1, ch], rot[:, z, ch], hl[:, 0, ch], ALU.subtract).then_inc(lo, 1)

        @block.gpsimd
        def _(pool):
            p = nc.gpsimd
            p.memset(V0[:], 0.0).then_inc(s_const, 1)
            for t, value in ((nm, 0.0), (nm3, 0.0), (MT, 0.0), (gp, -1.0), (ones_row, 1.0)):
                p.memset(t[:], value).then_inc(s_const, 1)
            pool.wait_ge(s_const, 6)
            p.memset(V0[:, :, :, HD0:HD0 + 1], 1.0).then_inc(s_const, 1)
            pool.wait_ge(loaded, 16 * n_c)

            def held(n):
                p.tensor_tensor(pspare[:, n:n + 1], x_sb[:, 0, 0:1], x_sb[:, 0, 1:2], ALU.mult)

            def chain2(b):
                n = [0]

                def link(ins):
                    n[0] += 1
                    ins.then_inc(pool2, 1)
                    pool.wait_ge(pool2, upto(b, POOL2, n[0]))
                yield from rotation(p, pool, 0, k_rot, k_hi, k_lo, khl, b, link)
                assert n[0] == POOL2, n[0]

            def chain3(b):
                yield 0
                pool.wait_ge(x2_ready, upto(b, 1))
                held(0)
                p.tensor_copy(x2r[:], x2[:]).then_inc(x2_kept, 1)
                for k in range(H // 2):
                    yield at_scores3(2 * k + 3) + 2
                    pool.wait_ge(pv3_kept, upto(b, H // 2, k + 1))
                    pair_sums = OL[:, (k + 1) * S:(k + 2) * S]
                    if k:
                        pool.wait_ge(sums3_added, upto(b, H // 2, k))
                        p.tensor_tensor(ssum[:], ssum[:], pair_sums, ALU.add).then_inc(sums3_added, 1)
                    else:
                        held(1)
                        p.tensor_copy(ssum[:], pair_sums).then_inc(sums3_added, 1)
                yield 84
                pool.wait_ge(y_ready, upto(b, 1))
                pool.dma_start(out[bass.ds(b, 1)].rearrange("a (t p) d -> p (a t) d", p=P), ln[3]["t"][:]).then_inc(stored, 16)
                pool.wait_ge(stored, b * 16 + 16)

            rounds(pool, lambda b: iter(()), chain2, chain3)

        @block.scalar
        def _(act):
            s = nc.scalar
            for n, (dst, src) in enumerate([(wk_eff[:, 0], PA[:, 0]), (wk_eff[:, 1], PA[:, 1]), (vo[:, 0:4], PB[:, 0]), (vo[:, 4:8], PB[:, 1]),
                                            (Wc[:, 0:4], PC[:, 0]), (Wc[:, 4:8], PC[:, 1]), (bc[:, 0:4], PAo[:]), (bc[:, 4:8], PCo[:])]):
                act.wait_ge(s_wprod, n + 1)
                s.copy(dst.rearrange("p g n -> p (g n)"), src).then_inc(s_wcopy, 1)
            act.wait_ge(loaded, 16 * n_c)
            act.wait_ge(s_const, 7)

            def chain1(b):
                yield 1.2
                act.wait_ge(xe_done, upto(b, 1))
                s.copy(xeT[:], PA[:, 0, 0:S]).then_inc(xeT_ready, 1)
                yield 2
                act.wait_ge(kproj, upto(b, 1))
                for g in range(G):
                    i = s.activation(K4[:, g, :], PA[0:96, g // 2, g % 2 * S:(g % 2 + 1) * S], ACT.Identity, bias=c["bk"][0:96, g:g + 1])
                i.then_inc(k_high, 1)
                yield 5
                act.wait_ge(qproj, upto(b, 1))
                for g in range(G):
                    i = s.activation(Q4[0:96, g, :], PA[0:96, g // 2, g % 2 * S:(g % 2 + 1) * S], ACT.Identity, bias=c["bq"][0:96, g:g + 1])
                i.then_inc(q_high, 1)
                yield at_smax(H) + 1
                act.wait_ge(nmT, upto(b, 1))
                s.copy(Q4[96:P, :, :], PA[96:P, 0, 0:S].unsqueeze(1).to_broadcast([32, G, S])).then_inc(nmT_kept, 1)
                for h in range(H):
                    yield at_scores(h) + 0.5
                    act.wait_ge(scores, upto(b, H, h + 1))
                    if h >= 8:
                        act.wait_ge(pv, upto(b, G, h // 4 - 1))
                    s.activation(Pr[:, h % 8, :], PA[:, h % 2, :], ACT.Exp, scale=SCALE0).then_inc(probs, 1)
                    if h == 9 or h == H - 1:
                        if h == H - 1:
                            yield at_scores(H) + 1
                        k = h // 10
                        act.wait_ge(pv, upto(b, G, 2 * k + 2))
                        s.copy(U[:, 512 * k:512 * k + 512], PAo[:]).then_inc(pv_kept, 1)

            def chain2(b):
                yield 1
                act.wait_ge(x1T_done, upto(b, 1))
                s.copy(x1T[:], PB[:, 0, 0:S]).then_inc(x1T_kept, 1)
                yield 2.5
                act.wait_ge(gate_shifted, upto(b, 1))
                s.activation(ge[:], lg[:], ACT.Exp).then_inc(gate_exp, 1)
                for e in range(E):
                    yield at_expert(e) + 0.5
                    act.wait_ge(h_up, upto(b, E, e + 1))
                    if e >= 2:
                        act.wait_ge(y_done, upto(b, E, e - 1))
                    s.activation(th[:, e % 2, :], PB[:, 0, :], ACT.Tanh, scale=0.5).then_inc(h_tanh, 1)
                yield 44
                act.wait_ge(x2T_done, upto(b, 1))
                s.copy(x2T[:], PB[:, 0, 0:S]).then_inc(x2T_kept, 1)
                yield 45
                act.wait_ge(latp, upto(b, 1))
                s.copy(lat[:].rearrange("p t l -> p (t l)"), PB[:, 0, 0:T * LAT]).then_inc(lat_kept, 1)
                for ch in range(2):
                    for z in range(2):
                        yield at_proj(2 * ch + z) + 1
                        act.wait_ge(proj, upto(b, 4, 2 * ch + z + 1))
                        if ch:
                            act.wait_ge((k_rot, q_rot)[z], upto(b, 2, 1))
                        s.copy(raw[:, z].rearrange("p e n -> p (e n)"), PB[:].rearrange("p a n -> p (a n)")).then_inc(raw_kept, 1)
                    yield at_turn(1, 3 * ch + 2)
                    for rotated, hi, hl, z in ((k_rot, k_hi, khl, 0), (q_rot, q_hi, qhl, 1)):
                        act.wait_ge(rotated, upto(b, 2, ch + 1))
                        s.copy(hl[:, 0, ch], rot[:, z, ch]).then_inc(hi, 1)

            def chain3(b):
                yield 0
                act.wait_ge(lat_kept, upto(b, 1))
                s.copy(lat3[:], lat[:]).then_inc(lat3_kept, 1)
                yield at_smax3(H) + 1
                act.wait_ge(nm3T, upto(b, 1))
                s.copy(MT[0:32, :], PC[0:32, 0, 0:S]).then_inc(nm3T_kept, 1)
                for h in range(H + 3):
                    yield at_scores3(h) + 0.5
                    if h < H:
                        act.wait_ge(scores3, upto(b, H, h + 1))
                        if h >= 4:
                            act.wait_ge(pv3, upto(b, H // 2, h // 2 - 1))
                        s.activation(Pr3[:, h % 4, :], PC[:, h % 2, 0:384], ACT.Exp, scale=SCALE1).then_inc(probs3, 1)
                    if h >= 3 and h % 2:
                        k = h // 2 - 1
                        yield at_scores3(h) + 1
                        act.wait_ge(pv3, upto(b, H // 2, k + 1))
                        if k:
                            act.wait_ge(sums3_added, upto(b, H // 2, k))
                        s.copy(OL[:, k * S:(k + 2) * S], PCo[:]).then_inc(pv3_kept, 1)
                yield 78
                act.wait_ge(x3T_done, upto(b, 1))
                s.copy(x3T[:], PC[:, 0, 0:S]).then_inc(x3T_kept, 1)

            rounds(act, chain1, chain2, chain3)

        @block.vector
        def _(dve):
            v = nc.vector
            dve.wait_ge(loaded, 16 * n_c)
            v.tensor_copy(Km[96:P, :, :, :].rearrange("p g j s -> p (g j) s"),
                          c["onehot0"][96:P, :].unsqueeze(2).to_broadcast([32, H, S])).then_inc(s_onehot, 1)
            dve.wait_ge(s_const, 7)
            dve.wait_ge(s_wcopy, 8)

            def linker(own, total, b):
                n = [0]

                def link(ins):
                    n[0] += 1
                    ins.then_inc(own, 1)
                    dve.wait_ge(own, upto(b, total, n[0]))
                link.n = n
                return link

            def held():
                v.memset(spare[:], 0.0)

            def rows(t):
                return t[:].unsqueeze(1).to_broadcast([P, T, D])

            def two_d(bank):
                return bank[:, 0:T * D].rearrange("p (t d) -> p t d", t=T)

            def layer_norm(k, link, src, dst):
                m = ln[k]
                for t in range(T):
                    i = v.bn_stats(m["st"][:, t], src[:, t])
                link(i)
                held()
                for t in range(T):
                    i = v.bn_aggr(m["mv"][:, t], m["st"][:, t])
                link(i)
                w, r, u = m["w"][:], m["r"][:], m["u"][:]
                link(v.tensor_scalar(w, m["mv"][:, :, 1], LN_EPS, None, ALU.add))
                link(v.tensor_scalar(r.bitcast(I32), w.bitcast(I32), 1, None, ALU.arith_shift_right))
                link(v.tensor_scalar(r.bitcast(I32), r.bitcast(I32), -1.0, RSQRT_BITS, ALU.mult, ALU.add))
                for _ in range(3):
                    link(v.scalar_tensor_tensor(out=u, in0=r, scalar=-0.5, in1=r, op0=ALU.mult, op1=ALU.mult))
                    link(v.tensor_tensor(u, u, w, ALU.mult))
                    link(v.scalar_tensor_tensor(out=r, in0=u, scalar=1.5, in1=r, op0=ALU.add, op1=ALU.mult))
                for t in range(T):
                    i = v.tensor_scalar(dst[:, t], src[:, t], m["mv"][:, t, 0:1], m["r"][:, t:t + 1], ALU.subtract, ALU.mult)
                return i

            def chain1(b):
                link = linker(dve1, DVE1, b)
                yield 0
                v.tensor_tensor(xe[:], x_sb[:, bass.ds(b * T, T), :], pe_sb[:], ALU.add).then_inc(xe_ready, 1)
                yield 3
                dve.wait_ge(k_high, upto(b, 1))
                for g in range(G):
                    i = v.scalar_tensor_tensor(out=K4[32:64, g, :], in0=PA[32:64, g // 2, g % 2 * S:(g % 2 + 1) * S],
                                               scalar=c["bk"][32:64, g:g + 1], in1=K4[32:64, g, :],
                                               op0=ALU.add, op1=ALU.subtract)
                i.then_inc(k_low, 1)
                dve.wait_ge(k_low, upto(b, 1))
                for j in range(4):
                    i = v.tensor_scalar(Km[0:96, :, j, :], K4[:], c["hmask"][0:96, j:j + 1], None, ALU.mult)
                i.then_inc(heads_masked, 1)
                yield 6
                dve.wait_ge(q_high, upto(b, 1))
                for g in range(G):
                    i = v.scalar_tensor_tensor(out=Q4[64:96, g, :], in0=PA[64:96, g // 2, g % 2 * S:(g % 2 + 1) * S],
                                               scalar=c["bq"][64:96, g:g + 1], in1=Q4[64:96, g, :],
                                               op0=ALU.add, op1=ALU.subtract)
                i.then_inc(q_split, 1)
                dve.wait_ge(vproj, upto(b, 1))
                v.tensor_tensor(V0[:, :, :, 0:HD0], PAo[:, 0:T * D].rearrange("p (t h d) -> p t h d", t=T, d=HD0),
                                    c["bv_b"][:].rearrange("p (h d) -> p h d", d=HD0).unsqueeze(1).to_broadcast([P, T, H, HD0]),
                                    ALU.add).then_inc(v_kept, 1)
                for h in range(H):
                    yield at_smax(h) + 0.5
                    dve.wait_ge(smax, upto(b, H, h + 1))
                    v.reduce_max(mx[:, :, h], PA[:, h % 2, :].rearrange("p (t k) -> p t k", t=T), AX.X).then_inc(smax_read, 1)
                yield at_smax(H)
                dve.wait_ge(smax_read, upto(b, H))
                v.tensor_scalar(nm[:, :, 0:H], mx[:], -1.0, None, ALU.mult).then_inc(nm_ready, 1)
                yield at_scores(H) + 2
                dve.wait_ge(sums, upto(b, 1))
                v.reciprocal(rsum[:], PA[:, 0, 0:S]).then_inc(rsum_ready, 1)
                yield at_scores(H) + 3
                dve.wait_ge(sums_back, upto(b, 1))
                v.tensor_tensor(U[:], U[:], PA[:].rearrange("p a n -> p (a n)"), ALU.mult).then_inc(att_ready, 1)
                yield at_scores(H) + 5
                s_, t_ = ln[1]["s"], ln[1]["t"]
                dve.wait_ge(wo_done, upto(b, 1))
                link(v.tensor_tensor(s_[:], two_d(PA[:, 0]), xe[:], ALU.add))
                link(v.tensor_tensor(s_[:], s_[:], rows(c["bo_b"]), ALU.add))
                link(layer_norm(1, link, s_, t_))
                yield at_scores(H) + 7
                link(v.tensor_tensor(t_[:], t_[:], rows(c["gamma_b"]), ALU.mult))
                link(v.tensor_tensor(t_[:], t_[:], rows(c["beta_b"]), ALU.add))
                link(v.tensor_tensor(s_[:], t_[:], x_sb[:, bass.ds(b * T, T), :], ALU.add))
                yield at_scores(H) + 8
                layer_norm(1, link, s_, x1).then_inc(x1_ready, 1)
                assert link.n[0] == DVE1, link.n

            def chain2(b):
                link = linker(dve2, DVE2, b)
                yield 2
                dve.wait_ge(logits, upto(b, 1))
                lgp = PB[:, 1, 0:T * E].rearrange("p (t e) -> p t e", t=T)
                link(v.reduce_max(lmx[:], lgp, AX.X))
                v.tensor_tensor(lg[:], lgp, lmx[:].unsqueeze(2).to_broadcast([P, T, E]), ALU.subtract).then_inc(gate_shifted, 1)
                yield 3
                dve.wait_ge(gate_exp, upto(b, 1))
                link(v.reduce_sum(gs[:], ge[:], AX.X))
                link(v.reciprocal(gs[:], gs[:]))
                link(v.tensor_tensor(gp[:, :, 0:E], ge[:], gs[:].unsqueeze(2).to_broadcast([P, T, E]), ALU.mult))
                held()
                for t in range(T):
                    i = v.max(top[:, t], gp[:, t, 0:E])
                link(i)
                link(v.memset(top[:, :, 2:8], -1.0))
                held()
                for t in range(T):
                    i = v.match_replace(gr[:, t], top[:, t], gp[:, t], -2.0)
                link(i)
                link(v.tensor_tensor(gr[:, :, 0:E], gr[:, :, 0:E], gp[:, :, 0:E], ALU.not_equal))
                link(v.tensor_tensor(cw[:], gr[:, :, 0:E], gp[:, :, 0:E], ALU.mult))
                link(v.reduce_sum(gs[:], cw[:], AX.X))
                link(v.tensor_scalar(gs[:], gs[:], GATE_EPS, None, ALU.max))
                link(v.reciprocal(gs[:], gs[:]))
                link(v.tensor_tensor(cw[:], cw[:], gs[:].unsqueeze(2).to_broadcast([P, T, E]), ALU.mult))
                link(v.tensor_scalar(cw[:], cw[:], 0.5, None, ALU.mult))
                for e in range(E + 1):
                    if e < E:
                        yield at_expert(e) + 1
                        dve.wait_ge(h_tanh, upto(b, E, e + 1))
                        v.scalar_tensor_tensor(out=th[:, e % 2, :], in0=th[:, e % 2, :], scalar=1.0, in1=PB[:, 0, :],
                                                   op0=ALU.add, op1=ALU.mult).then_inc(h_ready, 1)
                    if e:
                        yield at_expert(e) + 1.5
                        dve.wait_ge(y_done, upto(b, E, e))
                        if e > 1:
                            dve.wait_ge(y_added, upto(b, E, e - 1))
                        for t in range(T):
                            i = v.scalar_tensor_tensor(out=y[:, e % 2, t], in0=PB[:, 1, t * D:(t + 1) * D],
                                                       scalar=cw[:, t, e - 1:e],
                                                       in1=(y[:, (e + 1) % 2, t] if e > 1 else x1[:, t]),
                                                       op0=ALU.mult, op1=ALU.add)
                        i.then_inc(y_added, 1)
                yield at_expert(E) + 2
                dve.wait_ge(y_added, upto(b, E))
                if later(b):
                    dve.wait_ge(x2_kept, upto(b - 1, 1))
                layer_norm(2, link, y[:, E % 2], x2).then_inc(x2_ready, 1)
                yield from rotation(v, dve, 1, q_rot, q_hi, q_lo, qhl, b, link)
                assert link.n[0] == DVE2, link.n

            def chain3(b):
                link = linker(dve3, DVE3, b)
                for h in range(H):
                    yield at_smax3(h) + 0.5
                    dve.wait_ge(smax3, upto(b, H, h + 1))
                    v.reduce_max(mx3[:, h, :], PC[:, h % 2, 0:384].rearrange("p (t k) -> p t k", t=3), AX.X).then_inc(smax3_read, 1)
                yield at_smax3(H)
                dve.wait_ge(smax3_read, upto(b, H))
                v.tensor_scalar(nm3[:, 0, 0:H], mx3[:, :, 0], -1.0, None, ALU.mult)
                link(v.tensor_tensor(mx3[:, :, 1], mx3[:, :, 1], mx3[:, :, 2], ALU.max))
                v.tensor_scalar(nm3[:, 1, 0:H], mx3[:, :, 1], -1.0, None, ALU.mult).then_inc(nm3_ready, 1)
                yield at_scores3(H) + 5
                dve.wait_ge(sums3_added, upto(b, H // 2))
                v.reciprocal(ssum[:], ssum[:]).then_inc(rsum3_ready, 1)
                for k in range(4):
                    yield at_scores3(H) + 7 + k
                    dve.wait_ge(sums3_back, upto(b, 4, k + 1))
                    ol = OL[:, 2 * k * S:2 * (k + 1) * S]
                    v.tensor_tensor(ol, ol, PC[:, k % 2, :], ALU.mult).then_inc(ol_ready, 1)
                yield 76
                s_ = ln[3]["s"]
                dve.wait_ge(wo1_done, upto(b, 1))
                dve.wait_ge(x2_kept, upto(b, 1))
                link(v.tensor_tensor(s_[:], two_d(PC[:, 0]), x2r[:], ALU.add))
                layer_norm(3, link, s_, x3).then_inc(x3_ready, 1)
                yield 80
                dve.wait_ge(ffn, upto(b, 1))
                dve.wait_ge(x3_ready, upto(b, 1))
                link(v.tensor_tensor(s_[:], two_d(PC[:, 1]), x3[:], ALU.add))
                link(v.tensor_tensor(s_[:], s_[:], bc[:, bass.ds(b, 1), :].to_broadcast([P, T, D]), ALU.add))
                layer_norm(3, link, s_, ln[3]["t"]).then_inc(y_ready, 1)
                assert link.n[0] == DVE3, link.n

            rounds(dve, chain1, chain2, chain3)

        @block.tensor
        def _(pe):
            mm = nc.tensor.matmul
            pe.wait_ge(w_loaded, 16 * len(w_src))
            pe.wait_ge(s_const, 7)
            for f in range(2):
                mm(PA[:, f, :], kvd, kup[:, 512 * f:512 * f + 512], start=True, stop=True).then_inc(s_wprod, 1)
            for q in range(2):
                for p in range(4 * q, 4 * q + 4):
                    for hh in range(2):
                        r = slice(64 * hh, 64 * hh + 64)
                        i = mm(PB[r, q, p % 4 * D:(p % 4 + 1) * D], vup[r, p, :], wo1[r, p, :], start=True, stop=True)
                i.then_inc(s_wprod, 1)
            for q in range(2):
                for g in range(4 * q, 4 * q + 4):
                    for o in range(OCH):
                        i = mm(PC[:, q, g % 4 * D:(g % 4 + 1) * D], W1[:, g * OCH + o, :], W2T[:, g * OCH + o, :],
                               start=o == 0, stop=o == OCH - 1)
                i.then_inc(s_wprod, 1)
            for q in range(2):
                for g in range(4 * q, 4 * q + 4):
                    region = (PAo, PCo)[q][:, g % 4 * D:(g % 4 + 1) * D]
                    for o in range(OCH):
                        mm(region, b1[:, g * OCH + o:g * OCH + o + 1].to_broadcast([P, P]), W2T[:, g * OCH + o, :], start=o == 0, stop=False)
                    i = mm(region, ones_row[0:1, :], b2[0:1, g * D:(g + 1) * D], start=False, stop=True)
                i.then_inc(s_wprod, 1)
            pe.wait_ge(loaded, 16 * n_c)
            pe.wait_ge(s_onehot, 1)
            pe.wait_ge(s_wcopy, 8)

            def transposed(bank, src):
                for t in range(T):
                    i = nc.tensor.transpose(bank[:, t * P:(t + 1) * P], src[:, t], ident[:])
                return i

            def chain1(b):
                yield 1
                pe.wait_ge(xe_ready, upto(b, 1))
                transposed(PA[:, 0], xe).then_inc(xe_done, 1)
                yield 1.5
                pe.wait_ge(xeT_ready, upto(b, 1))
                for g in range(G):
                    i = mm(PA[0:96, g // 2, g % 2 * S:(g % 2 + 1) * S], c["wk3"][:, g, :], xeT[:], start=True, stop=True)
                i.then_inc(kproj, 1)
                for t in range(T):
                    i = mm(PAo[:, t * D:(t + 1) * D], xeT[:, t * P:(t + 1) * P], c["wv0"][:], start=True, stop=True)
                i.then_inc(vproj, 1)
                yield 4
                pe.wait_ge(k_low, upto(b, 1))
                for g in range(G):
                    i = mm(PA[0:96, g // 2, g % 2 * S:(g % 2 + 1) * S], c["wq3"][:, g, :], xeT[:], start=True, stop=True)
                i.then_inc(qproj, 1)
                for h in range(H):
                    yield at_smax(h)
                    if h == 0:
                        pe.wait_ge(heads_masked, upto(b, 1))
                        pe.wait_ge(q_split, upto(b, 1))
                    if h >= 2:
                        pe.wait_ge(smax_read, upto(b, H, h - 1))
                    for t in range(T):
                        i = mm(PA[:, h % 2, t * S:(t + 1) * S], Q4[0:96, h // 4, t * P:(t + 1) * P], Km[0:96, h // 4, h % 4, :],
                               start=True, stop=True)
                    i.then_inc(smax, 1)
                yield at_smax(H) + 0.5
                pe.wait_ge(nm_ready, upto(b, 1))
                for t in range(T):
                    i = mm(PA[96:P, 0, t * P:(t + 1) * P], nm[:, t, :], i16[:], start=True, stop=True, tile_position=(0, 96))
                i.then_inc(nmT, 1)
                for h in range(H + 1):
                    yield at_scores(h)
                    if h == 0:
                        pe.wait_ge(nmT_kept, upto(b, 1))
                        pe.wait_ge(v_kept, upto(b, 1))
                    if h >= 2 and h < H:
                        pe.wait_ge(probs, upto(b, H, h - 1))
                    if h < H:
                        for k in range(T):
                            i = mm(PA[:, h % 2, k * S:(k + 1) * S], Km[:, h // 4, h % 4, k * P:(k + 1) * P], Q4[:, h // 4, :],
                                   start=True, stop=True)
                        i.then_inc(scores, 1)
                    g = {5: 0, 9: 1, 13: 2, 16: 3}.get(h)
                    if g is not None:
                        pe.wait_ge(probs, upto(b, H, 4 * g + 4))
                        if g == 2:
                            pe.wait_ge(pv_kept, upto(b, 2, 1))
                        for k in range(T):
                            for j in range(4):
                                hd = 4 * g + j
                                i = mm(PAo[32 * j:32 * j + 32, g % 2 * S:(g % 2 + 1) * S], V0[:, k, hd, :],
                                       Pr[:, hd % 8, k * S:(k + 1) * S], start=k == 0, stop=k == 1, tile_position=(0, 32 * j))
                        i.then_inc(pv, 1)
                yield at_scores(H) + 1.5
                pe.wait_ge(pv_kept, upto(b, 2))
                for g in range(G):
                    i = mm(PA[:, 0, 0:S], c["sumsel"][:, g, :], U[:, g * S:(g + 1) * S], start=g == 0, stop=g == G - 1)
                i.then_inc(sums, 1)
                yield at_scores(H) + 2.5
                pe.wait_ge(rsum_ready, upto(b, 1))
                for g in range(G):
                    for j in range(4):
                        i = mm(PA[32 * j:32 * j + 32, g // 2, g % 2 * S:(g % 2 + 1) * S],
                               ident[:, 4 * g + j:4 * g + j + 1].to_broadcast([P, 32]), rsum[:], start=True, stop=True,
                               tile_position=(0, 32 * j))
                i.then_inc(sums_back, 1)
                yield at_scores(H) + 4
                pe.wait_ge(att_ready, upto(b, 1))
                for t in range(T):
                    for g in range(G):
                        i = mm(PA[:, 0, t * D:(t + 1) * D], U[:, g * S + t * P:g * S + (t + 1) * P], c["wo0"][:, g, :],
                               start=g == 0, stop=g == G - 1)
                i.then_inc(wo_done, 1)

            def chain2(b):
                yield 0
                pe.wait_ge(x1_ready, upto(b, 1))
                transposed(PB[:, 0], x1).then_inc(x1T_done, 1)
                yield 1.5
                pe.wait_ge(x1T_kept, upto(b, 1))
                for t in range(T):
                    i = mm(PB[:, 1, t * E:(t + 1) * E], x1T[:, t * P:(t + 1) * P], c["router"][:], start=True, stop=True)
                i.then_inc(logits, 1)
                for e in range(E + 1):
                    yield at_expert(e)
                    if e < E:
                        if e:
                            pe.wait_ge(h_ready, upto(b, E, e))
                        for f in range(2):
                            i = mm(PB[:, 0, f * S:(f + 1) * S], c["w1"][:, e, f * P:(f + 1) * P], x1T[:], start=True, stop=True)
                        i.then_inc(h_up, 1)
                    if e:
                        yield at_expert(e) + 0.2
                        pe.wait_ge(h_ready, upto(b, E, e))
                        pe.wait_ge(gate_shifted, upto(b, 1))
                        if e > 1:
                            pe.wait_ge(y_added, upto(b, E, e - 1))
                        for t in range(T):
                            for f in range(2):
                                i = mm(PB[:, 1, t * D:(t + 1) * D], hT[:, (e - 1) % 2, f, t * P:(t + 1) * P], c["w2"][:, e - 1, f, :],
                                       start=f == 0, stop=f == 1)
                        i.then_inc(y_done, 1)
                yield 43
                pe.wait_ge(x2_ready, upto(b, 1))
                transposed(PB[:, 0], x2).then_inc(x2T_done, 1)
                yield 44.5
                pe.wait_ge(x2T_kept, upto(b, 1))
                for t in range(T):
                    i = mm(PB[:, 0, t * LAT:(t + 1) * LAT], x2T[:, t * P:(t + 1) * P], c["wkvT"][:], start=True, stop=True)
                i.then_inc(latp, 1)
                for n in range(4):
                    yield at_proj(n)
                    if n:
                        pe.wait_ge(raw_kept, upto(b, 4, n))
                    else:
                        pe.wait_ge(lat_kept, upto(b, 1))
                    for half in range(2):
                        for g in range(2):
                            i = mm(PB[:, half, g * S:(g + 1) * S], (wk_eff, c["wq1"])[n % 2][:, half, 2 * (n // 2) + g, :], x2T[:],
                                   start=True, stop=True)
                    i.then_inc(proj, 1)

            def chain3(b):
                yield 0
                pe.wait_ge(keys_moved, b * 256 + 256)
                pe.wait_ge(queries_moved, b * 512 + 512)
                if later(b):
                    pe.wait_ge(y_ready, upto(b - 1, 1))
                for h in range(H):
                    yield at_smax3(h)
                    if h >= 2:
                        pe.wait_ge(smax3_read, upto(b, H, h - 1))
                    for t in range(T):
                        q, k, o = slice(t * P, (t + 1) * P), slice(0, (t + 1) * P), t * P
                        mm(PC[:, h % 2, o:o + (t + 1) * P], QH[:, h, q], KA[:, h, k], start=True, stop=False)
                        i = mm(PC[:, h % 2, o + t * P:o + (t + 1) * P], i16[:], c["future_k"][:], start=False, stop=True)
                    i.then_inc(smax3, 1)
                yield at_smax3(H) + 0.5
                pe.wait_ge(nm3_ready, upto(b, 1))
                for t in range(T):
                    i = mm(PC[0:32, 0, t * P:(t + 1) * P], nm3[:, t, :], i16[:], start=True, stop=True)
                i.then_inc(nm3T, 1)
                for h in range(H + 3):
                    yield at_scores3(h)
                    if h == 0:
                        pe.wait_ge(nm3T_kept, upto(b, 1))
                        pe.wait_ge(lat3_kept, upto(b, 1))
                    if h < H:
                        if h >= 2:
                            pe.wait_ge(probs3, upto(b, H, h - 1))
                        for k in range(T):
                            q, o, n = slice(k * P, S), k * S, S - k * P
                            region = PC[:, h % 2, o:o + n]
                            mm(region, KA[:, h, k * P:(k + 1) * P], QH[:, h, q], start=True, stop=False)
                            mm(region, KA[:, h, k * P:(k + 1) * P], QL[:, h, q], start=False, stop=False)
                            mm(region, i16[:, h:h + 1].to_broadcast([P, P]), MT[:, q], start=False, stop=False)
                            i = mm(PC[:, h % 2, o:o + P], i16[:], c["future_q"][:], start=False, stop=True)
                        i.then_inc(scores3, 1)
                    if h >= 3 and h % 2:
                        p = h // 2 - 1
                        yield at_scores3(h) + 0.2
                        pe.wait_ge(probs3, upto(b, H, 2 * p + 2))
                        if p:
                            pe.wait_ge(pv3_kept, upto(b, H // 2, p))
                        for col, stat in ((0, [lat3[:, 0], lat3[:, 1]]), (S, [c["pairsel"][:, p]] * 2)):
                            for k in range(T):
                                for hh in range(2):
                                    i = mm(PCo[64 * hh:64 * hh + 64, col + k * P:col + S], stat[k],
                                           Pr3[:, (2 * p + hh) % 4, k * S:k * S + S - k * P], start=k == 0, stop=k == 1,
                                           tile_position=(0, 64 * hh))
                        i.then_inc(pv3, 1)
                for k in range(4):
                    yield at_scores3(H) + 6 + k
                    pe.wait_ge(rsum3_ready, upto(b, 1))
                    if k >= 2:
                        pe.wait_ge(ol_ready, upto(b, 4, k - 1))
                    for hh in range(2):
                        for r in (0, 64):
                            row = r + 2 * k + hh
                            i = mm(PC[r:r + 64, k % 2, hh * S:(hh + 1) * S], ident[:, row:row + 1].to_broadcast([P, 64]),
                                   ssum[:], start=True, stop=True, tile_position=(0, r))
                    i.then_inc(sums3_back, 1)
                yield 75
                pe.wait_ge(ol_ready, upto(b, 4))
                for t in range(T):
                    for p in range(H // 2):
                        i = mm(PC[:, 0, t * D:(t + 1) * D], OL[:, p * S + t * P:p * S + (t + 1) * P], vo[:, p, :],
                               start=p == 0, stop=p == H // 2 - 1)
                i.then_inc(wo1_done, 1)
                yield 77
                pe.wait_ge(x3_ready, upto(b, 1))
                transposed(PC[:, 0], x3).then_inc(x3T_done, 1)
                yield 79
                pe.wait_ge(x3T_kept, upto(b, 1))
                for t in range(T):
                    i = mm(PC[:, 1, t * D:(t + 1) * D], x3T[:, t * P:(t + 1) * P],
                           Wc[:, bass.ds(b, 1), :].rearrange("p a n -> p (a n)"), start=True, stop=True)
                i.then_inc(ffn, 1)

            rounds(pe, chain1, chain2, chain3)


def layouts(i):
    f = np.float32
    asc = np.ascontiguousarray
    r = {}
    x = i["L0_attn_x"]
    r["x"] = asc(x.reshape(B * T, P, D).transpose(1, 0, 2))
    pe = i["L0_attn_pe"][0, :S]
    r["pe"] = asc(pe.reshape(T, P, D).transpose(1, 0, 2))

    def thrice(w):
        w = w.reshape(-1, G, 32)
        return asc(np.concatenate([w, w, w], axis=2))
    r["wq3"], r["wk3"] = thrice(i["L0_attn_wq"]), thrice(i["L0_attn_wk"])
    r["bq"] = asc(thrice(i["L0_attn_bq"][None])[0].T)
    r["bk"] = asc(thrice(i["L0_attn_bk"][None])[0].T)
    r["wv0"] = i["L0_attn_wv"]
    wo = np.zeros((4, 32, G, D), f)
    wo[:, :HD0] = i["L0_attn_wo"].reshape(G, 4, HD0, D).transpose(1, 2, 0, 3)
    r["wo0"] = wo.reshape(P, G, D)
    for n, k in (("bv_b", "L0_attn_bv"), ("bo_b", "L0_attn_bo"), ("gamma_b", "L0_attn_gamma"), ("beta_b", "L0_attn_beta")):
        r[n] = asc(np.broadcast_to(i[k][None], (P, D)))
    r["router"] = i["L0_ffn_router_w"]
    r["w1"] = asc(i["L0_ffn_w1"].transpose(1, 0, 2))
    r["w2"] = asc(i["L0_ffn_w2"].reshape(E, 2, P, D).transpose(2, 0, 1, 3))

    def halves(w):
        w = w.reshape(4, G, 2, 32, -1)
        return asc(w.transpose(4, 2, 1, 0, 3))
    r["wq1"] = halves(i["L1_attn_wq"]).reshape(D, 2, G, P)
    r["w_kup"] = halves(i["L1_attn_w_k_up"]).reshape(LAT, H * HD1)
    r["w_kvd"] = i["L1_attn_w_kv_down"]
    r["wkvT"] = asc(i["L1_attn_w_kv_down"].T)
    r["w_vup"] = asc(i["L1_attn_w_v_up"].reshape(H // 2, P, LAT).transpose(1, 0, 2))
    r["w_o1"] = asc(i["L1_attn_wo"].T.reshape(H // 2, P, D).transpose(1, 0, 2))
    r["W1"] = asc(i["L1_ffn_W1"].reshape(B, OCH, P, D).transpose(2, 0, 1, 3).reshape(P, B * OCH, D))
    r["W2T"] = asc(i["L1_ffn_W2"].reshape(B, D, OCH, P).transpose(3, 0, 2, 1).reshape(P, B * OCH, D))
    r["b1"] = asc(i["L1_ffn_b1"].reshape(B, OCH, P).transpose(2, 0, 1).reshape(P, B * OCH))
    r["b2"] = asc(i["L1_ffn_b2"].reshape(1, B * D))

    r["ident"] = np.eye(P, dtype=f)
    r["i16"] = np.eye(P, dtype=np.float16)
    hmask = np.zeros((P, 4), f)
    for j in range(4):
        for q in range(3):
            hmask[32 * q + 8 * j:32 * q + 8 * j + 8, j] = 1
    r["hmask"] = hmask
    one = np.zeros((P, H), np.float16)
    one[96 + np.arange(H), np.arange(H)] = 1
    r["onehot0"] = one
    sel = np.zeros((4, 32, G, P // H, G, 4), f)
    for j in range(4):
        for g in range(G):
            sel[j, HD0, g, :, g, j] = 1
    r["sumsel"] = sel.reshape(P, G, P)
    pair = np.zeros((H // 2, LAT), f)
    pair[np.arange(LAT) % (H // 2), np.arange(LAT)] = 1
    r["pairsel"] = asc(np.broadcast_to(pair, (P, H // 2, LAT)))
    q, k = np.indices((P, P))
    r["future_k"] = np.where(k > q, MASKED, 0).astype(np.float16)
    r["future_q"] = asc(r["future_k"].T)
    inv = (f(1.0) / (f(10000.0) ** (np.arange(0, HD1, 2, dtype=f) / f(HD1)))).astype(f)
    ang = (np.arange(S, dtype=f)[None] * inv[:, None]).astype(f)
    r["cos"] = asc(np.tile(np.cos(ang), (4, 1)))
    r["sin"] = asc(np.tile(np.sin(ang), (4, 1)))
    return r


def program(nc, arrays):
    args = {n: nc.dram_tensor(f"in_{n}", v.shape, mybir.dt.from_np(v.dtype), kind="ExternalInput").ap() for n, v in arrays.items()}
    out = nc.dram_tensor("out_0", (B, S, D), F32, kind="ExternalOutput").ap()
    build(nc, args, out)


def kernel(**inputs):
    import concourse.bacc as _bacc
    from concourse.bass_utils import run_bass_kernel_spmd as _run

    arrays = layouts({k: np.asarray(v) for k, v in inputs.items()})
    nc = _bacc.Bacc("TRN2", target_bir_lowering=False, num_devices=1)
    program(nc, arrays)
    r = _run(nc, [{f"in_{n}": v for n, v in arrays.items()}], core_ids=[0])
    return r.results[0]["out_0"]
```

```python
from contextlib import ExitStack

import numpy as np

import concourse.bass as bass
from concourse import mybir

F32 = mybir.dt.float32
F16 = mybir.dt.float16
I32 = mybir.dt.int32
ALU = mybir.AluOpType
ACT = mybir.ActivationFunctionType
AX = mybir.AxisListType

B, S, D = 8, 256, 128
P = 128
T = S // P
H = 16
HD0, HD1 = 8, 64
G = H // 4
E, FI = 8, 256
LAT = 64
OCH = 4
LN_EPS, GATE_EPS = 1e-5, 1e-9
SCALE0, SCALE1 = HD0 ** -0.5, HD1 ** -0.5
RSQRT_BITS = float(0x5F3759DF)
ORDER = {
    "pe": "121434124421421212232114211421311212112132112312121211313231313113131113231233231323313331"
          "233323330330333333303333333",
    "act": "22222222422232212112112112112111111112212323333322333323033303333233303333333",
    "dve": "412441244112222422444444444144214443112141121141414144124434444424433233332222323222222222"
           "23332333312122111111111111111012111211112101111211102",
    "pool": "222222423222232323232323330",
}
DVE1, DVE2, DVE3, POOL2 = 34, 33, 33, 6
W_UNIT = 2.0 ** -8
SUM_UNIT = 2.0 ** -8
MASKED = -60000.0


def together(order, **parts):
    for chain in parts.values():
        next(chain, None)
    for step in order:
        if "chain" + step in parts:
            next(parts["chain" + step], None)


def build(nc, a, out):
    ctx = ExitStack()
    with ctx:
        def sb(name, shape, dt=F32):
            return ctx.enter_context(nc.sbuf_tensor(name, shape, dt))

        def ps(name, shape):
            return ctx.enter_context(nc.psum_tensor(name, shape, F32))

        def sem(name):
            return ctx.enter_context(nc.semaphore(name))

        x_sb = sb("x_sb", [P, B * T, D])
        pe_sb = sb("pe_sb", [P, T, D])
        once = ("w_kup", "w_vup", "w_o1", "w_kvd", "W1", "W2T", "b1", "b2", "w1", "wq1")
        c = {n: sb("c_" + n, list(v.shape), v.dtype) for n, v in a.items()
             if n not in ("x", "pe") + once}
        ident, i16 = c["ident"], c["i16"]
        wk2 = sb("wk2", [P, 2, 2, G, P], F16)
        vo = sb("vo", [P, H // 2, D])
        Wc = sb("Wc", [P, B, D])
        bc = sb("bc", [P, B, D])
        w1s = sb("w1s", [P, 2, E, FI], F16)
        wq2 = sb("wq2", [P, 2, 2, G, P], F16)

        xeT = sb("xeT", [P, S])
        xe = sb("xe", [P, T, D])
        K4 = sb("K4", [96, G, S], F16)
        Q4 = sb("Q4", [P, G, S], F16)
        Km = sb("Km", [P, G, 4, S], F16)
        V0 = sb("V0", [P, T, H, 32])
        mx = sb("mx", [P, T, H])
        nm = sb("nm", [P, T, 32], F16)
        Pr = sb("Pr", [P, 8, 512])
        U = sb("U", [P, G * S])
        rsum = sb("rsum", [P, S])
        rhi = sb("rhi", [P, S], F16)
        rsplit = sb("rsplit", [P, S], F16)
        x1 = sb("x1", [P, T, D])
        x1T = x2T = sb("x12T", [P, S])
        x1s = x2s = sb("x12s", [P, 2, S], F16)
        lg = sb("lg", [P, T, 8])
        lmx = sb("lmx", [P, T])
        ge = sb("ge", [P, T, 8])
        gp = sb("gp", [P, T, 16])
        top = sb("top", [P, T, 8])
        gr = sb("gr", [P, T, 16])
        gs = sb("gs", [P, T])
        cw = sb("cw", [P, T, 8])
        hT = sb("hT", [P, 2, 2, S])
        th = hT[:].rearrange("p e c s -> p e (c s)")
        y = sb("y", [P, 2, T, D])
        ysum = sb("ysum", [P, T, D])
        x2 = sb("x2", [P, T, D])
        lat = sb("lat", [P, T, LAT])
        C2 = G * S // 2
        raw = sb("raw", [P, 2, 2, C2])
        rot = sb("rot", [P, 2, 2, 2, C2])
        rtm = sb("rtm", [P, 2, C2])
        khl = sb("khl", [P, 2, 2, 2, C2], F16)
        qhl = sb("qhl", [P, 2, 2, 2, C2], F16)
        KQ = sb("KQ", [P, 3, H, S], F16)
        KA = KQ[:, 0]
        QH = KQ[:, 1]
        QL = KQ[:, 2]
        x2r = sb("x2r", [P, T, D])
        lat3 = sb("lat3", [P, T, LAT])
        mx3 = sb("mx3", [P, H, 3])
        nm3 = sb("nm3", [P, T, 32], F16)
        MT = sb("MT", [P, S], F16)
        Pr3 = sb("Pr3", [P, 4, 384])
        OL = sb("OL", [P, (H // 2 + 1) * S])
        ssum = sb("ssum", [P, P])
        shi = sb("shi", [P, P], F16)
        ssplit = sb("ssplit", [P, P], F16)
        x3 = sb("x3", [P, T, D])
        x3T = sb("x3T", [P, S])
        ln = {n: {k: sb(f"{k}{n}", sh) for k, sh in (("s", [P, T, D]), ("t", [P, T, D]), ("st", [P, T, 6]), ("mv", [P, T, 2]),
                                                    ("w", [P, T]), ("r", [P, T]), ("u", [P, T]))} for n in (1, 2, 3)}
        spare, pspare = sb("spare", [P, 1]), sb("pspare", [P, 3])
        W1 = KQ[:, 0:2].bitcast(F32).rearrange("p a h (o n) -> p (a h o) n", n=D)
        W2T = rot[:].rearrange("p a b e (o n) -> p (a b e o) n", n=D)
        kup = OL[0:LAT, 0:H * HD1]
        wo1 = OL[:, 1024:2048].rearrange("p (h n) -> p h n", n=D)
        kvd = OL[0:LAT, 2048:2048 + D]
        vup = raw[:, 0, 0].rearrange("p (h n) -> p h n", n=LAT)
        b1 = raw[:, 0, 1, 0:B * OCH]
        b2 = Pr3[0:1].rearrange("p a n -> p (a n)")[:, 0:B * D]
        w1 = KQ[:, 2].bitcast(F32)
        wq1 = qhl[:, 0].rearrange("p a b n -> p (a b n)").bitcast(F32)
        ones_row = sb("ones_row", [1, P])

        PA, PAo = ps("PA", [P, 2, 512]), ps("PAo", [P, 512])
        PB = ps("PB", [P, 2, 512])
        PC, PCo = ps("PC", [P, 2, 512]), ps("PCo", [P, 512])

        first_loaded, w_loaded, loaded = sem("first_loaded"), sem("weights_to_multiply_loaded"), sem("loaded")
        s_const, s_onehot = sem("constants_set"), sem("onehot_rows_set")
        s_wprod, s_wcopy = sem("weight_products"), sem("weight_products_kept")
        w_high, w_low = sem("weights_high"), sem("weights_low")
        heads_moved, stored = [sem(f"heads_{4 * j}_on_moved") for j in range(4)], sem("stored")
        n_moves = 12

        def upto(b, per_row, n=None):
            return b * per_row + (per_row if n is None else n)

        def later(b):
            return not (isinstance(b, int) and b == 0)

        xe_ready, xe_done, xeT_ready, kproj, qproj = sem("xe_ready"), sem("xe_done"), sem("xeT_ready"), sem("kproj"), sem("qproj")
        vproj, k_high, q_high, k_low, heads_masked = sem("vproj"), sem("k_high"), sem("q_high"), sem("k_low"), sem("heads_masked")
        q_split, v_kept, biases_added = sem("q_split"), sem("v_kept"), sem("biases_added")
        smax, smax_read, nm_ready, nmT, nmT_kept = sem("smax"), sem("smax_read"), sem("nm_ready"), sem("nmT"), sem("nmT_kept")
        scores, probs, pv, pv_kept = sem("scores"), sem("probs"), sem("pv"), sem("pv_kept")
        sums, rsum_ready, sums_back, att_ready, wo_done = sem("sums"), sem("rsum_ready"), sem("sums_back"), sem("att_ready"), sem("wo_done")
        x1_ready, dve1 = sem("x1_ready"), sem("dve1")
        x1T_done, x1T_kept, logits, gate_shifted, gate_exp = sem("x1T_done"), sem("x1T_kept"), sem("logits"), sem("gate_shifted"), sem("gate_exp")
        x1_high, x1_low, x2_low = sem("x1_high"), sem("x1_low"), sem("x2_low")
        h_up, h_tanh, h_ready, y_done, y_added, y_weighted, cw_ready = sem("h_up"), sem("h_tanh"), sem("h_ready"), sem("y_done"), sem("y_added"), sem("y_weighted"), sem("cw_ready")
        x2_ready, x2T_done, x2T_kept, latp, lat_kept = sem("x2_ready"), sem("x2T_done"), sem("x2T_kept"), sem("latp"), sem("lat_kept")
        proj, raw_kept, k_rot, k_hi, k_lo = sem("proj"), sem("raw_kept"), sem("k_rot"), sem("k_hi"), sem("k_lo")
        q_rot, q_hi, q_lo, dve2, pool2 = sem("q_rot"), sem("q_hi"), sem("q_lo"), sem("dve2"), sem("pool2")
        x2_kept, lat3_kept, smax3, smax3_read, nm3_ready = sem("x2_kept"), sem("lat3_kept"), sem("smax3"), sem("smax3_read"), sem("nm3_ready")
        nm3T, nm3T_kept, scores3, probs3 = sem("nm3T"), sem("nm3T_kept"), sem("scores3"), sem("probs3")
        pv3, pv3_kept, sums3_added, rsum3_ready, sums3_back = sem("pv3"), sem("pv3_kept"), sem("sums3_added"), sem("rsum3_ready"), sem("sums3_back")
        ol_ready = sem("ol_ready")
        wo1_done, x3_ready, x3T_done, x3T_kept, ffn = sem("wo1_done"), sem("x3_ready"), sem("x3T_done"), sem("x3T_kept"), sem("ffn")
        y_ready, dve3, mx3_joined = sem("y_ready"), sem("dve3"), sem("mx3_joined")

        def rounds(eng, order, weights, chain0, chain1, chain2, chain3, chain4):
            together(order, chain0=chain0(0))
            together(order, chain1=chain1(0), chain0=chain0(1), chain2=weights())
            together(order, chain1=chain1(1), chain0=chain0(2), chain2=chain2(0))
            together(order, chain1=chain1(2), chain0=chain0(3), chain2=chain2(1), chain3=chain3(0))
            with eng.Fori(3, B - 1) as r:
                together(order, chain1=chain1(r), chain0=chain0(r + 1), chain2=chain2(r - 1), chain3=chain3(r - 2), chain4=chain4(r - 3))
            together(order, chain1=chain1(B - 1), chain2=chain2(B - 2), chain3=chain3(B - 3), chain4=chain4(B - 4))
            together(order, chain2=chain2(B - 1), chain3=chain3(B - 2), chain4=chain4(B - 3))
            together(order, chain3=chain3(B - 1), chain4=chain4(B - 2))
            together(order, chain4=chain4(B - 1))

        def nothing(b):
            return iter(())

        w_banks = [PB[:, 0], PB[:, 1], PC[:, 0], PC[:, 1], PCo[:], PB[:, 0], PB[:, 1], PC[:, 0]]

        block = ctx.enter_context(nc.Block())
        first = ["ident", "wk3", "bk", "hmask", "wv0", "onehot0", "wq3", "bq", "bv_b", "i16", "sumsel", "low0", "both0",
                 "wo0", "bo_b", "gamma_b", "beta_b"]
        n_first = 16 * (len(first) + 2)
        then = [n for n in c if n not in first]
        w_src = [(kup, "w_kup"), (kvd, "w_kvd"), (vup, "w_vup"), (wo1, "w_o1"), (W1, "W1"), (W2T, "W2T"), (b1, "b1"), (b2, "b2"), (w1, "w1"),
                 (wq1, "wq1")]

        @block.sync
        def _(sp):
            for dst, n in ((x_sb, "x"), (pe_sb, "pe")):
                sp.dma_start(dst[:], a[n]).then_inc(first_loaded, 16)
            for n in first:
                sp.dma_start(c[n][:], a[n]).then_inc(first_loaded, 16)
            for dst, n in w_src:
                sp.dma_start(dst, a[n]).then_inc(w_loaded, 16)
            for n in then:
                sp.dma_start(c[n][:], a[n]).then_inc(loaded, 16)

            def move_heads(b, first):
                for split in (k_hi, k_lo, q_hi, q_lo):
                    sp.wait_ge(split, upto(b, 2))
                for j in range(4):
                    if not first:
                        sp.wait_ge(scores3, upto(b - 1, H, 4 * j + 4))
                    for half in range(2):
                        for row, dst, src in ((0, KA, khl[:, 0]), (64, KA, khl[:, 1]), (0, QH, qhl[:, 0]), (64, QH, qhl[:, 0]),
                                              (0, QL, qhl[:, 1]), (64, QL, qhl[:, 1])):
                            r = row + 32 * half
                            sp.dma_start(dst[r:r + 32, 4 * j:4 * j + 4, :].rearrange("p (a g) n -> p a (g n)", a=2),
                                         src[32 * j:32 * j + 32, :, half, :]).then_inc(heads_moved[j], 16)

            move_heads(0, True)
            with sp.Fori(1, B) as b:
                move_heads(b, False)

        def rotation(eng, engine, z, rotated, hi, lo, hl, b, link):
            cosb = c["cos"][:].unsqueeze(1).to_broadcast([P, 2, S])
            sinb = c["sin"][:].unsqueeze(1).to_broadcast([P, 2, S])
            t = rtm[:, z].rearrange("p (g s) -> p g s", s=S)
            for ch in range(2):
                first, second = (raw[:, z, i].rearrange("p (g s) -> p g s", s=S) for i in range(2))
                out1, out2 = (rot[:, z, ch, i].rearrange("p (g s) -> p g s", s=S) for i in range(2))
                yield
                engine.wait_ge(raw_kept, upto(b, 4, 2 * ch + z + 1))
                eng.tensor_tensor(out1, first, cosb, ALU.mult)
                link(eng.tensor_tensor(t, second, sinb, ALU.mult))
                yield
                link(eng.tensor_tensor(out1, out1, t, ALU.subtract))
                eng.tensor_tensor(out2, second, cosb, ALU.mult)
                yield
                link(eng.tensor_tensor(t, first, sinb, ALU.mult))
                eng.tensor_tensor(out2, out2, t, ALU.add).then_inc(rotated, 1)
            for ch in range(2):
                yield
                engine.wait_ge(hi, upto(b, 2, ch + 1))
                eng.tensor_tensor(hl[:, 1, ch], rot[:, z, ch], hl[:, 0, ch], ALU.subtract).then_inc(lo, 1)

        @block.gpsimd
        def _(pool):
            p = nc.gpsimd
            p.memset(V0[:], 0.0).then_inc(s_const, 1)
            for t, value in ((nm, 0.0), (nm3, 0.0), (MT, 0.0), (gp, -1.0), (ones_row, 1.0)):
                p.memset(t[:], value).then_inc(s_const, 1)
            pool.wait_ge(s_const, 6)
            p.memset(V0[:, :, :, HD0:HD0 + 1], 1.0).then_inc(s_const, 1)
            pool.wait_ge(first_loaded, n_first)

            def weights():
                yield
                pool.wait_ge(loaded, 16 * len(then))
                held(2)

            def held(n):
                p.tensor_tensor(pspare[:, n:n + 1], pe_sb[:, 0, 0:1], pe_sb[:, 0, 1:2], ALU.mult)

            def chain0(b):
                yield
                pool.wait_ge(xe_done, upto(b, 1))
                p.tensor_tensor(xe[:], xe[:], c["bo_b"][:].unsqueeze(1).to_broadcast([P, T, D]), ALU.add).then_inc(biases_added, 1)
                x = x_sb[:, bass.ds(b * T, T), :]
                p.tensor_tensor(x, x, c["beta_b"][:].unsqueeze(1).to_broadcast([P, T, D]), ALU.add).then_inc(biases_added, 1)

            def chain2(b):
                n = [0]

                def link(ins):
                    n[0] += 1
                    ins.then_inc(pool2, 1)
                    pool.wait_ge(pool2, upto(b, POOL2, n[0]))
                for e in range(E):
                    yield
                    pool.wait_ge(y_weighted, upto(b, E, e + 1))
                    if e:
                        pool.wait_ge(y_added, upto(b, E, e))
                    elif later(b):
                        pool.wait_ge(x2_ready, upto(b - 1, 1))
                    p.tensor_tensor(ysum[:], (ysum if e else x1)[:], y[:, (e + 1) % 2], ALU.add).then_inc(y_added, 1)
                yield from rotation(p, pool, 0, k_rot, k_hi, k_lo, khl, b, link)
                assert n[0] == POOL2, n[0]

            def chain3(b):
                yield
                pool.wait_ge(x2_ready, upto(b, 1))
                held(0)
                p.tensor_copy(x2r[:], x2[:]).then_inc(x2_kept, 1)
                for k in range(H // 2):
                    yield
                    pool.wait_ge(pv3_kept, upto(b, H // 2, k + 1))
                    pair_sums = OL[:, (k + 1) * S:(k + 1) * S + P]
                    if k:
                        pool.wait_ge(sums3_added, upto(b, H // 2, k))
                        p.tensor_tensor(ssum[:], ssum[:], pair_sums, ALU.add).then_inc(sums3_added, 1)
                    else:
                        held(1)
                        p.tensor_copy(ssum[:], pair_sums).then_inc(sums3_added, 1)

            def chain4(b):
                yield
                pool.wait_ge(y_ready, upto(b, 1))
                pool.dma_start(out[bass.ds(b, 1)].rearrange("a (t p) d -> p (a t) d", p=P), ln[3]["t"][:]).then_inc(stored, 16)
                pool.wait_ge(stored, b * 16 + 16)

            rounds(pool, ORDER["pool"], weights, chain0, nothing, chain2, chain3, chain4)

        @block.scalar
        def _(act):
            s = nc.scalar
            act.wait_ge(first_loaded, n_first)
            act.wait_ge(s_const, 7)

            def weights():
                for n, (dst, src) in enumerate([(w1s[:, 0].rearrange("p e n -> p (e n)"), w1), (wq2[:, 0].rearrange("p a g n -> p (a g n)"), wq1)]):
                    yield
                    act.wait_ge(w_loaded, 16 * len(w_src))
                    s.activation(dst, src, ACT.Identity, scale=1 / W_UNIT).then_inc(w_high, 1)
                for n, src in enumerate(w_banks):
                    yield
                    act.wait_ge(s_wprod, n + 1)
                    if n < 2:
                        dst = wk2[:, 0, n].rearrange("p g n -> p (g n)")
                        s.activation(dst, src, ACT.Identity, scale=1 / W_UNIT).then_inc(s_wcopy, 1)
                    else:
                        dst = (vo, Wc, bc)[n // 2 - 1][:, n % 2 * 4:n % 2 * 4 + 4]
                        s.copy(dst.rearrange("p g n -> p (g n)"), src).then_inc(s_wcopy, 1)
                yield
                act.wait_ge(loaded, 16 * len(then))

            def chain0(b):
                yield
                act.wait_ge(xe_done, upto(b, 1))
                s.copy(xeT[:], PA[:, 0, 0:S]).then_inc(xeT_ready, 1)
                yield
                act.wait_ge(kproj, upto(b, 1))
                for g in range(G):
                    i = s.activation(K4[:, g, :], PA[0:96, g // 2, g % 2 * S:(g % 2 + 1) * S], ACT.Identity, bias=c["bk"][0:96, g:g + 1])
                i.then_inc(k_high, 1)
                yield
                act.wait_ge(qproj, upto(b, 1))
                for g in range(G):
                    i = s.activation(Q4[0:96, g, :], PA[0:96, g // 2, g % 2 * S:(g % 2 + 1) * S], ACT.Identity, bias=c["bq"][0:96, g:g + 1])
                i.then_inc(q_high, 1)

            def chain1(b):
                yield
                act.wait_ge(nmT, upto(b, 1))
                s.copy(Q4[96:P, :, :], PA[96:P, 0, 0:S].unsqueeze(1).to_broadcast([32, G, S])).then_inc(nmT_kept, 1)
                for h in range(H):
                    yield
                    act.wait_ge(scores, upto(b, H, h + 1))
                    if h >= 8:
                        act.wait_ge(pv, upto(b, G, h // 4 - 1))
                    s.activation(Pr[:, h % 8, :], PA[:, h % 2, :], ACT.Exp, scale=SCALE0).then_inc(probs, 1)
                    if h == 9 or h == H - 1:
                        if h == H - 1:
                            yield
                        k = h // 10
                        act.wait_ge(pv, upto(b, G, 2 * k + 2))
                        s.copy(U[:, 512 * k:512 * k + 512], PAo[:]).then_inc(pv_kept, 1)

            def chain2(b):
                yield
                act.wait_ge(x1T_done, upto(b, 1))
                s.copy(x1T[:], PB[:, 0, 0:S]).then_inc(x1T_kept, 1)
                s.copy(x1s[:, 0], PB[:, 0, 0:S]).then_inc(x1_high, 1)
                yield
                act.wait_ge(gate_shifted, upto(b, 1))
                s.activation(ge[:], lg[:], ACT.Exp).then_inc(gate_exp, 1)
                for e in range(E + 1):
                    if e < E:
                        yield
                        act.wait_ge(h_up, upto(b, E, e + 1))
                        if e >= 2:
                            act.wait_ge(y_done, upto(b, E, e - 1))
                        s.activation(th[:, e % 2, :], PB[:, 0, :], ACT.Tanh, scale=0.5 * W_UNIT).then_inc(h_tanh, 1)
                    if e:
                        yield
                        act.wait_ge(y_done, upto(b, E, e))
                        if e == 1:
                            act.wait_ge(cw_ready, upto(b, 1))
                        if e >= 3:
                            act.wait_ge(y_added, upto(b, E, e - 2))
                        for t in range(T):
                            i = s.activation(y[:, e % 2, t], PB[:, 1, t * D:(t + 1) * D], ACT.Identity, scale=cw[:, t, e - 1:e])
                        i.then_inc(y_weighted, 1)
                yield
                act.wait_ge(x2T_done, upto(b, 1))
                s.copy(x2s[:, 0], PB[:, 0, 0:S])
                s.copy(x2T[:], PB[:, 0, 0:S]).then_inc(x2T_kept, 1)
                yield
                act.wait_ge(latp, upto(b, 1))
                s.copy(lat[:].rearrange("p t l -> p (t l)"), PB[:, 1, 0:T * LAT]).then_inc(lat_kept, 1)
                for ch in range(2):
                    for z in range(2):
                        yield
                        act.wait_ge(proj, upto(b, 4, 2 * ch + z + 1))
                        if ch:
                            act.wait_ge((k_rot, q_rot)[z], upto(b, 2, 1))
                        s.copy(raw[:, z].rearrange("p e n -> p (e n)"), PB[:].rearrange("p a n -> p (a n)")).then_inc(raw_kept, 1)
                    yield
                    for rotated, hi, hl, z in ((k_rot, k_hi, khl, 0), (q_rot, q_hi, qhl, 1)):
                        act.wait_ge(rotated, upto(b, 2, ch + 1))
                        s.copy(hl[:, 0, ch], rot[:, z, ch]).then_inc(hi, 1)

            def chain3(b):
                yield
                act.wait_ge(lat_kept, upto(b, 1))
                s.copy(lat3[:], lat[:]).then_inc(lat3_kept, 1)
                yield
                act.wait_ge(nm3T, upto(b, 1))
                s.copy(MT[0:32, :], PC[0:32, 0, 0:S]).then_inc(nm3T_kept, 1)
                for h in range(H + 3):
                    yield
                    if h < H:
                        act.wait_ge(scores3, upto(b, H, h + 1))
                        if h >= 4:
                            act.wait_ge(pv3, upto(b, H // 2, h // 2 - 1))
                        s.activation(Pr3[:, h % 4, :], PC[:, h % 2, 0:384], ACT.Exp, scale=SCALE1).then_inc(probs3, 1)
                    if h >= 3 and h % 2:
                        k = h // 2 - 1
                        yield
                        act.wait_ge(pv3, upto(b, H // 2, k + 1))
                        if k:
                            act.wait_ge(sums3_added, upto(b, H // 2, k))
                        s.copy(OL[:, k * S:(k + 1) * S + P], PCo[:, 0:S + P]).then_inc(pv3_kept, 1)

            def chain4(b):
                yield
                act.wait_ge(x3T_done, upto(b, 1))
                s.copy(x3T[:], PAo[:, 0:S]).then_inc(x3T_kept, 1)

            rounds(act, ORDER["act"], weights, chain0, chain1, chain2, chain3, chain4)

        @block.vector
        def _(dve):
            v = nc.vector
            dve.wait_ge(first_loaded, n_first)
            v.tensor_copy(Km[96:P, :, :, :].rearrange("p g j s -> p (g j) s"),
                          c["onehot0"][96:P, :].unsqueeze(2).to_broadcast([32, H, S])).then_inc(s_onehot, 1)
            dve.wait_ge(s_const, 7)

            def weights():
                for n, (part, src) in enumerate([(w1s, w1), (wq2, wq1)]):
                    hi, lo = (part[:, k].rearrange("p a n -> p (a n)" if n == 0 else "p a g n -> p (a g n)") for k in range(2))
                    yield
                    dve.wait_ge(w_high, n + 1)
                    v.scalar_tensor_tensor(out=lo, in0=src, scalar=1 / W_UNIT, in1=hi, op0=ALU.mult, op1=ALU.subtract).then_inc(w_low, 1)
                for half in range(2):
                    yield
                    hi, lo = (wk2[:, k, half].rearrange("p g n -> p (g n)") for k in range(2))
                    dve.wait_ge(s_wcopy, half + 1)
                    v.scalar_tensor_tensor(out=lo, in0=w_banks[half], scalar=1 / W_UNIT, in1=hi, op0=ALU.mult, op1=ALU.subtract).then_inc(w_low, 1)
                yield
                dve.wait_ge(s_wcopy, len(w_banks))
                dve.wait_ge(loaded, 16 * len(then))
                held()

            def linker(own, total, b):
                n = [0]

                def link(ins):
                    n[0] += 1
                    ins.then_inc(own, 1)
                    dve.wait_ge(own, upto(b, total, n[0]))
                link.n = n
                return link

            def held():
                v.memset(spare[:], 0.0)

            def rows(t):
                return t[:].unsqueeze(1).to_broadcast([P, T, D])

            def two_d(bank):
                return bank[:, 0:T * D].rearrange("p (t d) -> p t d", t=T)

            def layer_norm(k, link, src, dst):
                m = ln[k]
                for t in range(T):
                    i = v.bn_stats(m["st"][:, t], src[:, t])
                link(i)
                yield
                held()
                for t in range(T):
                    i = v.bn_aggr(m["mv"][:, t], m["st"][:, t])
                link(i)
                yield
                w, r, u = m["w"][:], m["r"][:], m["u"][:]
                link(v.tensor_scalar(w, m["mv"][:, :, 1], LN_EPS, None, ALU.add))
                yield
                link(v.tensor_scalar(r.bitcast(I32), w.bitcast(I32), 1, None, ALU.arith_shift_right))
                yield
                link(v.tensor_scalar(r.bitcast(I32), r.bitcast(I32), -1.0, RSQRT_BITS, ALU.mult, ALU.add))
                for _ in range(3):
                    yield
                    link(v.scalar_tensor_tensor(out=u, in0=r, scalar=-0.5, in1=r, op0=ALU.mult, op1=ALU.mult))
                    yield
                    link(v.tensor_tensor(u, u, w, ALU.mult))
                    yield
                    link(v.scalar_tensor_tensor(out=r, in0=u, scalar=1.5, in1=r, op0=ALU.add, op1=ALU.mult))
                yield
                for t in range(T):
                    i = v.tensor_scalar(dst[:, t], src[:, t], m["mv"][:, t, 0:1], m["r"][:, t:t + 1], ALU.subtract, ALU.mult)
                return i

            def chain0(b):
                yield
                v.tensor_tensor(xe[:], x_sb[:, bass.ds(b * T, T), :], pe_sb[:], ALU.add).then_inc(xe_ready, 1)
                yield
                dve.wait_ge(k_high, upto(b, 1))
                for g in range(G):
                    i = v.scalar_tensor_tensor(out=K4[32:64, g, :], in0=PA[32:64, g // 2, g % 2 * S:(g % 2 + 1) * S],
                                               scalar=c["bk"][32:64, g:g + 1], in1=K4[32:64, g, :],
                                               op0=ALU.add, op1=ALU.subtract)
                i.then_inc(k_low, 1)
                dve.wait_ge(k_low, upto(b, 1))
                for j in range(4):
                    i = v.tensor_scalar(Km[0:96, :, j, :], K4[:], c["hmask"][0:96, j:j + 1], None, ALU.mult)
                i.then_inc(heads_masked, 1)
                yield
                dve.wait_ge(q_high, upto(b, 1))
                for g in range(G):
                    i = v.scalar_tensor_tensor(out=Q4[64:96, g, :], in0=PA[64:96, g // 2, g % 2 * S:(g % 2 + 1) * S],
                                               scalar=c["bq"][64:96, g:g + 1], in1=Q4[64:96, g, :],
                                               op0=ALU.add, op1=ALU.subtract)
                i.then_inc(q_split, 1)
                dve.wait_ge(vproj, upto(b, 1))
                v.tensor_tensor(V0[:, :, :, 0:HD0], PAo[:, 0:T * D].rearrange("p (t h d) -> p t h d", t=T, d=HD0),
                                    c["bv_b"][:].rearrange("p (h d) -> p h d", d=HD0).unsqueeze(1).to_broadcast([P, T, H, HD0]),
                                    ALU.add).then_inc(v_kept, 1)

            def chain1(b):
                link = linker(dve1, DVE1, b)
                for h in range(H):
                    yield
                    dve.wait_ge(smax, upto(b, H, h + 1))
                    v.reduce_max(mx[:, :, h], PA[:, h % 2, :].rearrange("p (t k) -> p t k", t=T), AX.X).then_inc(smax_read, 1)
                yield
                dve.wait_ge(smax_read, upto(b, H))
                v.tensor_scalar(nm[:, :, 0:H], mx[:], -1.0, None, ALU.mult).then_inc(nm_ready, 1)
                yield
                dve.wait_ge(sums, upto(b, 1))
                link(v.reciprocal(rsum[:], PA[:, 0, 0:S]))
                link(v.tensor_copy(rhi[:], rsum[:]))
                v.scalar_tensor_tensor(out=rsplit[:], in0=rhi[:], scalar=c["low0"][:, 0:1], in1=rsum[:],
                                       op0=ALU.mult, op1=ALU.subtract).then_inc(rsum_ready, 1)
                yield
                dve.wait_ge(sums_back, upto(b, 1))
                v.tensor_tensor(U[:], U[:], PA[:].rearrange("p a n -> p (a n)"), ALU.mult).then_inc(att_ready, 1)
                yield
                s_, t_ = ln[1]["s"], ln[1]["t"]
                dve.wait_ge(wo_done, upto(b, 1))
                dve.wait_ge(biases_added, upto(b, 2))
                link(v.tensor_tensor(s_[:], two_d(PA[:, 0]), xe[:], ALU.add))
                link((yield from layer_norm(1, link, s_, t_)))
                yield
                link(v.tensor_tensor(t_[:], t_[:], rows(c["gamma_b"]), ALU.mult))
                link(v.tensor_tensor(s_[:], t_[:], x_sb[:, bass.ds(b * T, T), :], ALU.add))
                yield
                if later(b):
                    dve.wait_ge(y_added, upto(b - 1, E, 1))
                (yield from layer_norm(1, link, s_, x1)).then_inc(x1_ready, 1)
                assert link.n[0] == DVE1, link.n

            def chain2(b):
                link = linker(dve2, DVE2, b)
                yield
                dve.wait_ge(x1_high, upto(b, 1))
                v.tensor_tensor(x1s[:, 1], PB[:, 0, 0:S], x1s[:, 0], ALU.subtract).then_inc(x1_low, 1)
                yield
                dve.wait_ge(logits, upto(b, 1))
                lgp = PB[:, 1, 0:T * E].rearrange("p (t e) -> p t e", t=T)
                link(v.reduce_max(lmx[:], lgp, AX.X))
                v.tensor_tensor(lg[:], lgp, lmx[:].unsqueeze(2).to_broadcast([P, T, E]), ALU.subtract).then_inc(gate_shifted, 1)
                for e in range(E):
                    yield
                    dve.wait_ge(h_tanh, upto(b, E, e + 1))
                    v.scalar_tensor_tensor(out=th[:, e % 2, :], in0=th[:, e % 2, :], scalar=1.0, in1=PB[:, 0, :],
                                           op0=ALU.add, op1=ALU.mult).then_inc(h_ready, 1)
                    if e == 0:
                        yield
                        dve.wait_ge(gate_exp, upto(b, 1))
                        link(v.reduce_sum(gs[:], ge[:], AX.X))
                        link(v.reciprocal(gs[:], gs[:]))
                        link(v.tensor_tensor(gp[:, :, 0:E], ge[:], gs[:].unsqueeze(2).to_broadcast([P, T, E]), ALU.mult))
                        yield
                        held()
                        for t in range(T):
                            i = v.max(top[:, t], gp[:, t, 0:E])
                        link(i)
                        link(v.memset(top[:, :, 2:8], -1.0))
                        held()
                        for t in range(T):
                            i = v.match_replace(gr[:, t], top[:, t], gp[:, t], -2.0)
                        link(i)
                        yield
                        link(v.tensor_tensor(gr[:, :, 0:E], gr[:, :, 0:E], gp[:, :, 0:E], ALU.not_equal))
                        link(v.tensor_tensor(cw[:], gr[:, :, 0:E], gp[:, :, 0:E], ALU.mult))
                        link(v.reduce_sum(gs[:], cw[:], AX.X))
                        yield
                        link(v.tensor_scalar(gs[:], gs[:], GATE_EPS, None, ALU.max))
                        link(v.reciprocal(gs[:], gs[:]))
                        link(v.tensor_tensor(cw[:], cw[:], gs[:].unsqueeze(2).to_broadcast([P, T, E]), ALU.mult))
                        v.tensor_scalar(cw[:], cw[:], 0.5 * W_UNIT, None, ALU.mult).then_inc(cw_ready, 1)
                yield
                dve.wait_ge(y_added, upto(b, E))
                if later(b):
                    dve.wait_ge(x2_kept, upto(b - 1, 1))
                (yield from layer_norm(2, link, ysum, x2)).then_inc(x2_ready, 1)
                yield
                dve.wait_ge(x2T_kept, upto(b, 1))
                v.tensor_tensor(x2s[:, 1], PB[:, 0, 0:S], x2s[:, 0], ALU.subtract).then_inc(x2_low, 1)
                yield from rotation(v, dve, 1, q_rot, q_hi, q_lo, qhl, b, link)
                assert link.n[0] == DVE2, link.n

            def chain3(b):
                for h in range(H):
                    yield
                    dve.wait_ge(smax3, upto(b, H, h + 1))
                    v.reduce_max(mx3[:, h, :], PC[:, h % 2, 0:384].rearrange("p (t k) -> p t k", t=3), AX.X).then_inc(smax3_read, 1)
                yield
                dve.wait_ge(smax3_read, upto(b, H))
                v.tensor_scalar(nm3[:, 0, 0:H], mx3[:, :, 0], -1.0, None, ALU.mult)
                v.tensor_tensor(mx3[:, :, 1], mx3[:, :, 1], mx3[:, :, 2], ALU.max).then_inc(mx3_joined, 1)
                dve.wait_ge(mx3_joined, upto(b, 1))
                v.tensor_scalar(nm3[:, 1, 0:H], mx3[:, :, 1], -1.0, None, ALU.mult).then_inc(nm3_ready, 1)

            def chain4(b):
                link = linker(dve3, DVE3, b)
                yield
                dve.wait_ge(sums3_added, upto(b, H // 2))
                link(v.reciprocal(ssum[:], ssum[:]))
                link(v.tensor_copy(shi[:], ssum[:]))
                v.scalar_tensor_tensor(out=ssplit[:], in0=shi[:], scalar=c["low1"][:, 0:1], in1=ssum[:],
                                       op0=ALU.mult, op1=ALU.subtract).then_inc(rsum3_ready, 1)
                for k in range(4):
                    yield
                    dve.wait_ge(sums3_back, upto(b, 4, k + 1))
                    ol = OL[:, 2 * k * S:2 * (k + 1) * S]
                    v.tensor_tensor(ol, ol, (PCo, PAo)[k % 2][:], ALU.mult).then_inc(ol_ready, 1)
                yield
                s_ = ln[3]["s"]
                dve.wait_ge(wo1_done, upto(b, 1))
                dve.wait_ge(x2_kept, upto(b, 1))
                link(v.tensor_tensor(s_[:], two_d(PCo), x2r[:], ALU.add))
                (yield from layer_norm(3, link, s_, x3)).then_inc(x3_ready, 1)
                yield
                dve.wait_ge(ffn, upto(b, 1))
                dve.wait_ge(x3_ready, upto(b, 1))
                link(v.tensor_tensor(s_[:], two_d(PCo), x3[:], ALU.add))
                link(v.tensor_tensor(s_[:], s_[:], bc[:, bass.ds(b, 1), :].to_broadcast([P, T, D]), ALU.add))
                (yield from layer_norm(3, link, s_, ln[3]["t"])).then_inc(y_ready, 1)
                assert link.n[0] == DVE3, link.n

            rounds(dve, ORDER["dve"], weights, chain0, chain1, chain2, chain3, chain4)

        @block.tensor
        def _(pe):
            mm = nc.tensor.matmul
            pe.wait_ge(first_loaded, n_first)
            pe.wait_ge(s_onehot, 1)
            pe.wait_ge(s_const, 7)

            def weights():
                for n in range(2):
                    yield
                    pe.wait_ge(w_loaded, 16 * len(w_src))
                    mm(w_banks[n], kvd, kup[:, 512 * n:512 * n + 512], start=True, stop=True).then_inc(s_wprod, 1)
                for n in range(2, 4):
                    yield
                    for p in range(4 * n - 8, 4 * n - 4):
                        for hh in range(2):
                            r = slice(64 * hh, 64 * hh + 64)
                            i = mm(w_banks[n][r, p % 4 * D:(p % 4 + 1) * D], vup[r, p, :], wo1[r, p, :], start=True, stop=True)
                    i.then_inc(s_wprod, 1)
                for n in range(4, 6):
                    yield
                    if n == 5:
                        pe.wait_ge(w_low, 3)
                    for g in range(4 * n - 16, 4 * n - 12):
                        for o in range(OCH):
                            i = mm(w_banks[n][:, g % 4 * D:(g % 4 + 1) * D], W1[:, g * OCH + o, :], W2T[:, g * OCH + o, :],
                                   start=o == 0, stop=o == OCH - 1)
                    i.then_inc(s_wprod, 1)
                for n in range(6, 8):
                    yield
                    if n == 6:
                        pe.wait_ge(w_low, 4)
                    else:
                        pe.wait_ge(s_wcopy, 3)
                    for g in range(4 * n - 24, 4 * n - 20):
                        region = w_banks[n][:, g % 4 * D:(g % 4 + 1) * D]
                        for o in range(OCH):
                            mm(region, b1[:, g * OCH + o:g * OCH + o + 1].to_broadcast([P, P]), W2T[:, g * OCH + o, :], start=o == 0, stop=False)
                        i = mm(region, ones_row[0:1, :], b2[0:1, g * D:(g + 1) * D], start=False, stop=True)
                    i.then_inc(s_wprod, 1)
                yield
                pe.wait_ge(loaded, 16 * len(then))
                pe.wait_ge(s_wcopy, len(w_banks))
                pe.wait_ge(w_low, 4)

            def transposed(bank, src):
                for t in range(T):
                    i = nc.tensor.transpose(bank[:, t * P:(t + 1) * P], src[:, t], ident[:])
                return i

            def chain0(b):
                yield
                pe.wait_ge(xe_ready, upto(b, 1))
                transposed(PA[:, 0], xe).then_inc(xe_done, 1)
                yield
                pe.wait_ge(xeT_ready, upto(b, 1))
                for g in range(G):
                    i = mm(PA[0:96, g // 2, g % 2 * S:(g % 2 + 1) * S], c["wk3"][:, g, :], xeT[:], start=True, stop=True)
                i.then_inc(kproj, 1)
                for t in range(T):
                    i = mm(PAo[:, t * D:(t + 1) * D], xeT[:, t * P:(t + 1) * P], c["wv0"][:], start=True, stop=True)
                i.then_inc(vproj, 1)
                yield
                pe.wait_ge(k_low, upto(b, 1))
                for g in range(G):
                    i = mm(PA[0:96, g // 2, g % 2 * S:(g % 2 + 1) * S], c["wq3"][:, g, :], xeT[:], start=True, stop=True)
                i.then_inc(qproj, 1)

            def chain1(b):
                for h in range(H):
                    yield
                    if h == 0:
                        pe.wait_ge(heads_masked, upto(b, 1))
                        pe.wait_ge(q_split, upto(b, 1))
                        pe.wait_ge(v_kept, upto(b, 1))
                    if h >= 2:
                        pe.wait_ge(smax_read, upto(b, H, h - 1))
                    for t in range(T):
                        i = mm(PA[:, h % 2, t * S:(t + 1) * S], Q4[0:96, h // 4, t * P:(t + 1) * P], Km[0:96, h // 4, h % 4, :],
                               start=True, stop=True)
                    i.then_inc(smax, 1)
                yield
                pe.wait_ge(nm_ready, upto(b, 1))
                for t in range(T):
                    i = mm(PA[96:P, 0, t * P:(t + 1) * P], nm[:, t, :], i16[:], start=True, stop=True, tile_position=(0, 96))
                i.then_inc(nmT, 1)
                for h in range(H + 1):
                    yield
                    if h == 0:
                        pe.wait_ge(nmT_kept, upto(b, 1))
                    if h >= 2 and h < H:
                        pe.wait_ge(probs, upto(b, H, h - 1))
                    if h < H:
                        for k in range(T):
                            i = mm(PA[:, h % 2, k * S:(k + 1) * S], Km[:, h // 4, h % 4, k * P:(k + 1) * P], Q4[:, h // 4, :],
                                   start=True, stop=True)
                        i.then_inc(scores, 1)
                    g = {5: 0, 9: 1, 13: 2, 16: 3}.get(h)
                    if g is not None:
                        pe.wait_ge(probs, upto(b, H, 4 * g + 4))
                        if g == 2:
                            pe.wait_ge(pv_kept, upto(b, 2, 1))
                        for k in range(T):
                            for j in range(4):
                                hd = 4 * g + j
                                i = mm(PAo[32 * j:32 * j + 32, g % 2 * S:(g % 2 + 1) * S], V0[:, k, hd, :],
                                       Pr[:, hd % 8, k * S:(k + 1) * S], start=k == 0, stop=k == 1, tile_position=(0, 32 * j))
                        i.then_inc(pv, 1)
                yield
                pe.wait_ge(pv_kept, upto(b, 2))
                for g in range(G):
                    i = mm(PA[:, 0, 0:S], c["sumsel"][:, g, :], U[:, g * S:(g + 1) * S], start=g == 0, stop=g == G - 1)
                i.then_inc(sums, 1)
                yield
                pe.wait_ge(rsum_ready, upto(b, 1))
                for g in range(G):
                    for j in range(4):
                        i = mm(PA[32 * j:32 * j + 32, g // 2, g % 2 * S:(g % 2 + 1) * S],
                               c["both0"][:, 4 * g + j:4 * g + j + 1].to_broadcast([P, 32]), rsplit[:], start=True, stop=True,
                               tile_position=(0, 32 * j))
                i.then_inc(sums_back, 1)
                yield
                pe.wait_ge(att_ready, upto(b, 1))
                for t in range(T):
                    for g in range(G):
                        i = mm(PA[:, 0, t * D:(t + 1) * D], U[:, g * S + t * P:g * S + (t + 1) * P], c["wo0"][:, g, :],
                               start=g == 0, stop=g == G - 1)
                i.then_inc(wo_done, 1)

            def split_product(region, w, x):
                for wp, xp in ((0, 0), (1, 0), (0, 1)):
                    i = mm(region, w[:, wp], x[:, xp], start=wp + xp == 0, stop=xp == 1)
                return i

            def chain2(b):
                yield
                pe.wait_ge(x1_ready, upto(b, 1))
                transposed(PB[:, 0], x1).then_inc(x1T_done, 1)
                yield
                pe.wait_ge(x1T_kept, upto(b, 1))
                for t in range(T):
                    i = mm(PB[:, 1, t * E:(t + 1) * E], x1T[:, t * P:(t + 1) * P], c["router"][:], start=True, stop=True)
                i.then_inc(logits, 1)
                for e in range(E + 1):
                    yield
                    if e < E:
                        if e:
                            pe.wait_ge(h_ready, upto(b, E, e))
                        else:
                            pe.wait_ge(x1_low, upto(b, 1))
                        for f in range(2):
                            i = split_product(PB[:, 0, f * S:(f + 1) * S], w1s[:, :, e, f * P:(f + 1) * P], x1s)
                        i.then_inc(h_up, 1)
                    if e:
                        yield
                        pe.wait_ge(h_ready, upto(b, E, e))
                        pe.wait_ge(gate_shifted, upto(b, 1))
                        if e > 1:
                            pe.wait_ge(y_weighted, upto(b, E, e - 1))
                        for t in range(T):
                            for f in range(2):
                                i = mm(PB[:, 1, t * D:(t + 1) * D], hT[:, (e - 1) % 2, f, t * P:(t + 1) * P], c["w2"][:, e - 1, f, :],
                                       start=f == 0, stop=f == 1)
                        i.then_inc(y_done, 1)
                yield
                pe.wait_ge(x2_ready, upto(b, 1))
                transposed(PB[:, 0], x2).then_inc(x2T_done, 1)
                yield
                pe.wait_ge(x2T_kept, upto(b, 1))
                for t in range(T):
                    i = mm(PB[:, 1, t * LAT:(t + 1) * LAT], x2T[:, t * P:(t + 1) * P], c["wkvT"][:], start=True, stop=True)
                i.then_inc(latp, 1)
                for n in range(4):
                    yield
                    if n:
                        pe.wait_ge(raw_kept, upto(b, 4, n))
                    else:
                        pe.wait_ge(lat_kept, upto(b, 1))
                        pe.wait_ge(x2_low, upto(b, 1))
                    for half in range(2):
                        for g in range(2):
                            i = split_product(PB[:, half, g * S:(g + 1) * S], (wk2, wq2)[n % 2][:, :, half, 2 * (n // 2) + g, :], x2s)
                    i.then_inc(proj, 1)

            def chain3(b):
                yield
                for h in range(H):
                    yield
                    if h % 4 == 0:
                        pe.wait_ge(heads_moved[h // 4], 16 * upto(b, n_moves))
                    if h >= 2:
                        pe.wait_ge(smax3_read, upto(b, H, h - 1))
                    for t in range(T):
                        q, k, o = slice(t * P, (t + 1) * P), slice(0, (t + 1) * P), t * P
                        mm(PC[:, h % 2, o:o + (t + 1) * P], QH[:, h, q], KA[:, h, k], start=True, stop=False)
                        i = mm(PC[:, h % 2, o + t * P:o + (t + 1) * P], i16[:], c["future_k"][:], start=False, stop=True)
                    i.then_inc(smax3, 1)
                yield
                pe.wait_ge(nm3_ready, upto(b, 1))
                for t in range(T):
                    i = mm(PC[0:32, 0, t * P:(t + 1) * P], nm3[:, t, :], i16[:], start=True, stop=True)
                i.then_inc(nm3T, 1)
                for h in range(H + 3):
                    yield
                    if h == 0:
                        pe.wait_ge(nm3T_kept, upto(b, 1))
                        pe.wait_ge(lat3_kept, upto(b, 1))
                    if h < H:
                        if h >= 2:
                            pe.wait_ge(probs3, upto(b, H, h - 1))
                        for k in range(T):
                            q, o, n = slice(k * P, S), k * S, S - k * P
                            region = PC[:, h % 2, o:o + n]
                            mm(region, KA[:, h, k * P:(k + 1) * P], QH[:, h, q], start=True, stop=False)
                            mm(region, KA[:, h, k * P:(k + 1) * P], QL[:, h, q], start=False, stop=False)
                            mm(region, i16[:, h:h + 1].to_broadcast([P, P]), MT[:, q], start=False, stop=False)
                            i = mm(PC[:, h % 2, o:o + P], i16[:], c["future_q"][:], start=False, stop=True)
                        i.then_inc(scores3, 1)
                    if h >= 3 and h % 2:
                        p = h // 2 - 1
                        yield
                        pe.wait_ge(probs3, upto(b, H, 2 * p + 2))
                        if p:
                            pe.wait_ge(pv3_kept, upto(b, H // 2, p))
                        elif later(b):
                            pe.wait_ge(y_ready, upto(b - 1, 1))
                        for k in range(T):
                            for hh in range(2):
                                mm(PCo[64 * hh:64 * hh + 64, k * P:S], lat3[:, k],
                                   Pr3[:, (2 * p + hh) % 4, k * S:k * S + S - k * P], start=k == 0, stop=k == 1,
                                   tile_position=(0, 64 * hh))
                        for k, q in ((0, 0), (0, 1), (1, 1)):
                            for hh in range(2):
                                r, o = 32 * (2 * hh + q), (k + q) * P
                                i = mm(PCo[r:r + 32, S:S + P], c["pairsel"][:, p], Pr3[:, (2 * p + hh) % 4, o:o + P],
                                       start=k == 0, stop=k == q, tile_position=(0, r))
                        i.then_inc(pv3, 1)

            def chain4(b):
                for k in range(4):
                    yield
                    pe.wait_ge(rsum3_ready, upto(b, 1))
                    if k >= 2:
                        pe.wait_ge(ol_ready, upto(b, 4, k - 1))
                    for pp in range(2):
                        for q in range(T):
                            for hh in range(2):
                                n, o = (2 * hh + q) * (H // 2) + 2 * k + pp, (T * pp + q) * P
                                i = mm((PCo, PAo)[k % 2][64 * hh:64 * hh + 64, o:o + P], c["both1"][:, n:n + 1].to_broadcast([P, 64]),
                                       ssplit[:], start=True, stop=True, tile_position=(0, 64 * hh))
                    i.then_inc(sums3_back, 1)
                yield
                pe.wait_ge(ol_ready, upto(b, 4))
                for t in range(T):
                    for p in range(H // 2):
                        i = mm(PCo[:, t * D:(t + 1) * D], OL[:, p * S + t * P:p * S + (t + 1) * P], vo[:, p, :],
                               start=p == 0, stop=p == H // 2 - 1)
                i.then_inc(wo1_done, 1)
                yield
                pe.wait_ge(x3_ready, upto(b, 1))
                transposed(PAo, x3).then_inc(x3T_done, 1)
                yield
                pe.wait_ge(x3T_kept, upto(b, 1))
                for t in range(T):
                    i = mm(PCo[:, t * D:(t + 1) * D], x3T[:, t * P:(t + 1) * P],
                           Wc[:, bass.ds(b, 1), :].rearrange("p a n -> p (a n)"), start=True, stop=True)
                i.then_inc(ffn, 1)

            rounds(pe, ORDER["pe"], weights, chain0, chain1, chain2, chain3, chain4)


def layouts(i):
    f = np.float32
    asc = np.ascontiguousarray
    r = {}
    x = i["L0_attn_x"]
    r["x"] = asc(x.reshape(B * T, P, D).transpose(1, 0, 2))
    pe = i["L0_attn_pe"][0, :S]
    r["pe"] = asc(pe.reshape(T, P, D).transpose(1, 0, 2))

    def thrice(w):
        w = w.reshape(-1, G, 32)
        return asc(np.concatenate([w, w, w], axis=2))
    r["wq3"], r["wk3"] = thrice(i["L0_attn_wq"]), thrice(i["L0_attn_wk"])
    r["bq"] = asc(thrice(i["L0_attn_bq"][None])[0].T)
    r["bk"] = asc(thrice(i["L0_attn_bk"][None])[0].T)
    r["wv0"] = i["L0_attn_wv"]
    wo = np.zeros((4, 32, G, D), f)
    wo[:, :HD0] = i["L0_attn_wo"].reshape(G, 4, HD0, D).transpose(1, 2, 0, 3)
    r["wo0"] = wo.reshape(P, G, D)
    for n, k in (("bv_b", "L0_attn_bv"), ("bo_b", "L0_attn_bo"), ("gamma_b", "L0_attn_gamma"), ("beta_b", "L0_attn_beta")):
        r[n] = asc(np.broadcast_to(i[k][None], (P, D)))
    r["router"] = i["L0_ffn_router_w"]
    r["w1"] = asc(i["L0_ffn_w1"].transpose(1, 0, 2)).reshape(D, E * FI)
    r["w2"] = asc(i["L0_ffn_w2"].reshape(E, 2, P, D).transpose(2, 0, 1, 3))

    def halves(w):
        w = w.reshape(4, G, 2, 32, -1)
        return asc(w.transpose(4, 2, 1, 0, 3))
    r["wq1"] = halves(i["L1_attn_wq"]).reshape(D, 2 * G * P)
    r["w_kup"] = halves(i["L1_attn_w_k_up"]).reshape(LAT, H * HD1)
    r["w_kvd"] = i["L1_attn_w_kv_down"]
    r["wkvT"] = asc(i["L1_attn_w_kv_down"].T)
    r["w_vup"] = asc(i["L1_attn_w_v_up"].reshape(H // 2, P, LAT).transpose(1, 0, 2))
    r["w_o1"] = asc(i["L1_attn_wo"].T.reshape(H // 2, P, D).transpose(1, 0, 2))
    r["W1"] = asc(i["L1_ffn_W1"].reshape(B, OCH, P, D).transpose(2, 0, 1, 3).reshape(P, B * OCH, D))
    r["W2T"] = asc(i["L1_ffn_W2"].reshape(B, D, OCH, P).transpose(3, 0, 2, 1).reshape(P, B * OCH, D))
    r["b1"] = asc(i["L1_ffn_b1"].reshape(B, OCH, P).transpose(2, 0, 1).reshape(P, B * OCH))
    r["b2"] = asc(i["L1_ffn_b2"].reshape(1, B * D))

    r["ident"] = np.eye(P, dtype=f)
    r["i16"] = np.eye(P, dtype=np.float16)
    hmask = np.zeros((P, 4), f)
    for j in range(4):
        for q in range(3):
            hmask[32 * q + 8 * j:32 * q + 8 * j + 8, j] = 1
    r["hmask"] = hmask
    one = np.zeros((P, H), np.float16)
    one[96 + np.arange(H), np.arange(H)] = 1
    r["onehot0"] = one
    sel = np.zeros((4, 32, G, P // H, G, 4), f)
    for j in range(4):
        for g in range(G):
            sel[j, HD0, g, :, g, j] = SUM_UNIT
    r["sumsel"] = sel.reshape(P, G, P)
    pair = np.zeros((H // 2, 32), f)
    pair[np.arange(32) % (H // 2), np.arange(32)] = SUM_UNIT
    r["pairsel"] = asc(np.broadcast_to(pair, (P, H // 2, 32)))
    r["low0"] = (np.arange(P) >= 64).astype(f).reshape(P, 1)
    r["low1"] = (np.arange(P) % 32 >= 16).astype(f).reshape(P, 1)
    both = np.zeros((P, H), np.float16)
    both[np.arange(H), np.arange(H)] = both[64 + np.arange(H), np.arange(H)] = -SUM_UNIT
    r["both0"] = both
    both = np.zeros((4, 32, 4, H // 2), np.float16)
    for j in range(4):
        for n in range(H // 2):
            both[j, n, j, n] = both[j, 16 + n, j, n] = -SUM_UNIT
    r["both1"] = both.reshape(P, 4 * (H // 2))
    q, k = np.indices((P, P))
    r["future_k"] = np.where(k > q, MASKED, 0).astype(np.float16)
    r["future_q"] = asc(r["future_k"].T)
    inv = (f(1.0) / (f(10000.0) ** (np.arange(0, HD1, 2, dtype=f) / f(HD1)))).astype(f)
    ang = (np.arange(S, dtype=f)[None] * inv[:, None]).astype(f)
    r["cos"] = asc(np.tile(np.cos(ang) * f(W_UNIT), (4, 1)))
    r["sin"] = asc(np.tile(np.sin(ang) * f(W_UNIT), (4, 1)))
    return r


def program(nc, arrays):
    args = {n: nc.dram_tensor(f"in_{n}", v.shape, mybir.dt.from_np(v.dtype), kind="ExternalInput").ap() for n, v in arrays.items()}
    out = nc.dram_tensor("out_0", (B, S, D), F32, kind="ExternalOutput").ap()
    build(nc, args, out)


def kernel(**inputs):
    import concourse.bacc as _bacc
    from concourse.bass_utils import run_bass_kernel_spmd as _run

    arrays = layouts({k: np.asarray(v) for k, v in inputs.items()})
    nc = _bacc.Bacc("TRN2", target_bir_lowering=False, num_devices=1)
    program(nc, arrays)
    r = _run(nc, [{f"in_{n}": v for n, v in arrays.items()}], core_ids=[0])
    return r.results[0]["out_0"]
```
